# Optimizing a Trainium2 kernel written in Bass

```python
import numpy as np
import jax
import jax.numpy as jnp

def _softmax(x, axis=-1):
    return jax.nn.softmax(x, axis=axis)

def _gelu(x):
    return jax.nn.gelu(x, approximate=True)

def _silu(x):
    return jax.nn.silu(x)

def _sigmoid(x):
    return jax.nn.sigmoid(x)

def _layernorm(x, axis=-1, eps=1e-05):
    m = jnp.mean(x, axis=axis, keepdims=True)
    v = jnp.var(x, axis=axis, keepdims=True)
    return (x - m) / jnp.sqrt(v + eps)

def _scatter_add(tgt, idx, src, axis=0):
    return tgt.at[idx].add(src)

def _segment_sum(src, seg, n):
    return jax.ops.segment_sum(src, seg, n)
kernel_name = 'mk_prb_d2_jaxref_r4_730af6'

def setup_inputs(seed: int=0):
    np.random.seed(seed)
    _w = jnp.asarray

    def _L0_attn_setup():
        import jax, jax.numpy as jnp
        import numpy as np
        CHUNK = 32
        key = jax.random.key(seed)
        ks = jax.random.split(key, 7)
        B, T, D = (4, 2048, 256)
        s = 1.0 / np.sqrt(D)
        return {'x': jax.random.normal(ks[0], (B, T, D), jnp.float32), 'W_q': jax.random.normal(ks[1], (D, D), jnp.float32) * s, 'W_k': jax.random.normal(ks[2], (D, D), jnp.float32) * s, 'W_v': jax.random.normal(ks[3], (D, D), jnp.float32) * s, 'W_g': jax.random.normal(ks[4], (D, D), jnp.float32) * s, 'W_o': jax.random.normal(ks[5], (D, D), jnp.float32) * s, 'log_decay': jax.random.normal(ks[6], (D,), jnp.float32) * 0.1}
    _L0_attn_in = _L0_attn_setup()

    def _L0_ffn_setup():
        import jax, jax.numpy as jnp
        import numpy as np
        B, S, D = (4, 1024, 256)
        E, H = (16, 128)
        key = jax.random.key(seed)
        k0, k1, k2, k3 = jax.random.split(key, 4)
        std = 1.0 / np.sqrt(D)
        input_tensor = jax.random.normal(k0, (B, S, D), dtype=jnp.float32)
        expert_sel = jax.random.normal(k1, (E, D), dtype=jnp.float32) * std
        keys = jax.random.normal(k2, (E, D, H), dtype=jnp.float32) * std
        values = jax.random.normal(k3, (E, H, D), dtype=jnp.float32) * (1.0 / np.sqrt(E * H))
        return {'input_tensor': input_tensor, 'expert_sel': expert_sel, 'keys': keys, 'values': values}
    _L0_ffn_in = _L0_ffn_setup()

    def _L1_attn_setup():
        import jax, jax.numpy as jnp
        import numpy as np
        B, S, D, M, TOPK = (4, 512, 256, 4, 2)

        def _linear_scan(x_scan, a):

            def combine(c1, c2):
                a1, x1 = c1
                a2, x2 = c2
                return (a1 * a2, a2 * x1 + x2)
            _, h = jax.lax.associative_scan(combine, (a, x_scan), axis=-2)
            return h
        key = jax.random.key(seed)
        ks = jax.random.split(key, 8)
        s = 1.0 / np.sqrt(D)
        return {'x': jax.random.normal(ks[0], (B, S, D), jnp.float32), 'Wg': jax.random.uniform(ks[1], (M, D, D), jnp.float32, -s, s), 'bg': jax.random.uniform(ks[2], (M, D), jnp.float32, -s, s), 'Wv': jax.random.uniform(ks[3], (M, D, D), jnp.float32, -s, s), 'bv': jax.random.uniform(ks[4], (M, D), jnp.float32, -s, s), 'Wd': jax.random.uniform(ks[5], (M, D, D), jnp.float32, -s, s), 'bd': jnp.ones((M, D), jnp.float32), 'gate_W': jax.random.uniform(ks[6], (D, M), jnp.float32, -s, s)}
    _L1_attn_in = _L1_attn_setup()

    def _L1_ffn_setup():
        import jax, jax.numpy as jnp
        import numpy as np
        D_MODEL = 256
        D_FF = 1024
        NUM_EXPERTS = 8
        key = jax.random.key(seed)
        ks = jax.random.split(key, 8)
        scale_in = 1.0 / np.sqrt(D_MODEL)
        scale_ff = 1.0 / np.sqrt(D_FF)
        x = jax.random.normal(ks[0], (4, 512, D_MODEL), dtype=jnp.float32)
        gate_w = jax.random.uniform(ks[1], (NUM_EXPERTS, D_MODEL), jnp.float32, -scale_in, scale_in)
        gate_b = jax.random.uniform(ks[2], (NUM_EXPERTS,), jnp.float32, -scale_in, scale_in)
        expert_bias = jnp.zeros((NUM_EXPERTS,), dtype=jnp.float32)
        w1 = jax.random.uniform(ks[3], (NUM_EXPERTS, D_MODEL, D_FF), jnp.float32, -scale_in, scale_in)
        b1 = jax.random.uniform(ks[4], (NUM_EXPERTS, D_FF), jnp.float32, -scale_in, scale_in)
        w2 = jax.random.uniform(ks[5], (NUM_EXPERTS, D_FF, D_MODEL), jnp.float32, -scale_ff, scale_ff)
        b2 = jax.random.uniform(ks[6], (NUM_EXPERTS, D_MODEL), jnp.float32, -scale_ff, scale_ff)
        return {'x': x, 'gate_w': gate_w, 'gate_b': gate_b, 'expert_bias': expert_bias, 'w1': w1, 'b1': b1, 'w2': w2, 'b2': b2}
    _L1_ffn_in = _L1_ffn_setup()
    _d = {'L0_attn_x': _L0_attn_in['x'], 'L0_attn_W_q': _L0_attn_in['W_q'], 'L0_attn_W_k': _L0_attn_in['W_k'], 'L0_attn_W_v': _L0_attn_in['W_v'], 'L0_attn_W_g': _L0_attn_in['W_g'], 'L0_attn_W_o': _L0_attn_in['W_o'], 'L0_attn_log_decay': _L0_attn_in['log_decay'], 'L0_ffn_expert_sel': _L0_ffn_in['expert_sel'], 'L0_ffn_keys': _L0_ffn_in['keys'], 'L0_ffn_values': _L0_ffn_in['values'], 'L1_attn_Wg': _L1_attn_in['Wg'], 'L1_attn_bg': _L1_attn_in['bg'], 'L1_attn_Wv': _L1_attn_in['Wv'], 'L1_attn_bv': _L1_attn_in['bv'], 'L1_attn_Wd': _L1_attn_in['Wd'], 'L1_attn_bd': _L1_attn_in['bd'], 'L1_attn_gate_W': _L1_attn_in['gate_W'], 'L1_ffn_gate_w': _L1_ffn_in['gate_w'], 'L1_ffn_gate_b': _L1_ffn_in['gate_b'], 'L1_ffn_expert_bias': _L1_ffn_in['expert_bias'], 'L1_ffn_w1': _L1_ffn_in['w1'], 'L1_ffn_b1': _L1_ffn_in['b1'], 'L1_ffn_w2': _L1_ffn_in['w2'], 'L1_ffn_b2': _L1_ffn_in['b2']}
    _x0 = _d['L0_attn_x']
    _d['L0_attn_x'] = jax.random.normal(jax.random.fold_in(jax.random.key(seed), 1), (1, 4096, 256), dtype=_x0.dtype)
    del _x0
    return _d

def reference(L0_attn_x, L0_attn_W_q, L0_attn_W_k, L0_attn_W_v, L0_attn_W_g, L0_attn_W_o, L0_attn_log_decay, L0_ffn_expert_sel, L0_ffn_keys, L0_ffn_values, L1_attn_Wg, L1_attn_bg, L1_attn_Wv, L1_attn_bv, L1_attn_Wd, L1_attn_bd, L1_attn_gate_W, L1_ffn_gate_w, L1_ffn_gate_b, L1_ffn_expert_bias, L1_ffn_w1, L1_ffn_b1, L1_ffn_w2, L1_ffn_b2):

    def _L0_attn_ref(x, W_q, W_k, W_v, W_g, W_o, log_decay):
        import jax, jax.numpy as jnp
        import numpy as np
        CHUNK = 32
        B, T, D = x.shape
        C = CHUNK
        nc = T // C
        Q = x @ W_q.T
        K = x @ W_k.T
        V = x @ W_v.T
        decay = jax.lax.stop_gradient(jax.nn.sigmoid(log_decay[0]))
        pos = jnp.arange(C, dtype=x.dtype)
        diff = pos[:, None] - pos[None, :]
        mask = jnp.where(diff >= 0, decay ** diff, jnp.zeros((), x.dtype))
        Qc = Q.reshape(B, nc, C, D)
        Kc = K.reshape(B, nc, C, D)
        Vc = V.reshape(B, nc, C, D)
        S = jnp.einsum('bncd,bnkd->bnck', Qc, Kc) * mask
        O = jnp.einsum('bnck,bnkd->bncd', S, Vc).reshape(B, T, D)
        gate = jax.nn.sigmoid(x @ W_g.T)
        out = gate * O @ W_o.T + x
        return out

    def _L0_ffn_ref(input_tensor, expert_sel, keys, values):
        import jax, jax.numpy as jnp
        import numpy as np
        B, S, D = (4, 1024, 256)
        E, H = (16, 128)
        sel = jax.nn.sigmoid(jnp.einsum('bsd,ed->bse', input_tensor, expert_sel))
        scores = jax.nn.relu(jnp.einsum('bsd,edh->bseh', input_tensor, keys))
        out = jnp.einsum('bseh,ehv,bse->bsv', scores, values, sel)
        return out

    def _L1_attn_ref(x, Wg, bg, Wv, bv, Wd, bd, gate_W):
        import jax, jax.numpy as jnp
        import numpy as np
        B, S, D, M, TOPK = (4, 512, 256, 4, 2)

        def _linear_scan(x_scan, a):

            def combine(c1, c2):
                a1, x1 = c1
                a2, x2 = c2
                return (a1 * a2, a2 * x1 + x2)
            _, h = jax.lax.associative_scan(combine, (a, x_scan), axis=-2)
            return h
        gate_logits = jnp.einsum('bsd,dm->bsm', x, gate_W)
        top_vals, top_idx = jax.lax.top_k(gate_logits, TOPK)
        weights = jax.nn.softmax(top_vals, axis=-1)
        g = jnp.einsum('bsd,mde->mbse', x, Wg) + bg[:, None, None, :]
        v = jnp.einsum('bsd,mde->mbse', x, Wv) + bv[:, None, None, :]
        d = jnp.einsum('bsd,mde->mbse', x, Wd) + bd[:, None, None, :]
        x_scan = jax.nn.sigmoid(g) * jnp.tanh(v)
        a = 0.001 + 0.998 * jax.nn.sigmoid(d)
        h = _linear_scan(x_scan, a)
        comb = jnp.sum(jax.nn.one_hot(top_idx, M, dtype=x.dtype) * weights[..., None], axis=-2)
        return jnp.einsum('bsm,mbsd->bsd', comb, h)

    def _L1_ffn_ref(x, gate_w, gate_b, expert_bias, w1, b1, w2, b2):
        import jax, jax.numpy as jnp
        import numpy as np
        D_MODEL = 256
        D_FF = 1024
        NUM_EXPERTS = 8
        gate_logits = jnp.einsum('bsd,ed->bse', x, gate_w) + gate_b + expert_bias
        top_idx = jnp.argmax(gate_logits, axis=-1)
        out = jnp.zeros_like(x)
        for e in range(NUM_EXPERTS):
            mask = (top_idx == e)[..., None].astype(x.dtype)
            h = jax.nn.relu(jnp.einsum('bsd,df->bsf', x, w1[e]) + b1[e])
            y = jnp.einsum('bsf,fd->bsd', h, w2[e]) + b2[e]
            out = out + mask * y
        return out
    x = L0_attn_x
    xn = _layernorm(x, axis=-1)
    x = x + _L0_attn_ref(xn, L0_attn_W_q, L0_attn_W_k, L0_attn_W_v, L0_attn_W_g, L0_attn_W_o, L0_attn_log_decay) + _L0_ffn_ref(xn, L0_ffn_expert_sel, L0_ffn_keys, L0_ffn_values)
    xn = _layernorm(x, axis=-1)
    x = x + _L1_attn_ref(xn, L1_attn_Wg, L1_attn_bg, L1_attn_Wv, L1_attn_bv, L1_attn_Wd, L1_attn_bd, L1_attn_gate_W) + _L1_ffn_ref(xn, L1_ffn_gate_w, L1_ffn_gate_b, L1_ffn_expert_bias, L1_ffn_w1, L1_ffn_b1, L1_ffn_w2, L1_ffn_b2)
    return x

_drawn_inputs = setup_inputs


def setup_inputs(seed=0):
    import zlib

    import numpy as np

    out = dict(_drawn_inputs(seed))
    spreads = {'L1_attn_bd': (1.0, 0.6), 'L1_ffn_expert_bias': (0.0, 0.668)}
    factors = {'L0_ffn_expert_sel': 4.044,
     'L1_attn_Wg': 21.438,
     'L1_attn_bg': 200.0,
     'L1_attn_bv': 8.0,
     'L1_attn_Wd': 21.481,
     'L1_attn_gate_W': 3.233,
     'L1_ffn_gate_w': 2.777,
     'L1_ffn_gate_b': 8.0,
     'L1_ffn_w1': 3.189,
     'L1_ffn_b1': 43.356,
     'L1_ffn_b2': 33.162}
    for name, (base, spread) in spreads.items():
        noise = np.random.default_rng([zlib.crc32(name.encode()), seed]).standard_normal(out[name].shape)
        drawn = base * np.exp(spread * noise) if base else spread * noise
        out[name] = jnp.asarray(drawn.astype(out[name].dtype))
    for name, factor in factors.items():
        out[name] = (out[name] * factor).astype(out[name].dtype)
    return out
```

```python
import numpy as np
import concourse.bass as bass
from concourse import mybir

F32 = mybir.dt.float32
F32R = mybir.dt.float32r
I32 = mybir.dt.int32
U32 = mybir.dt.uint32
ALU = mybir.AluOpType
ACT = mybir.ActivationFunctionType
AX = mybir.AxisListType

P = 128
T, D = 4096, 256
DC = D // P
GT = 512
GROUPS = T // GT
JT = GT // P
TILES = T // P
E0, H0 = 16, 128
M = 4
MC = M * DC
E1, F1 = 8, 1024
FJ = F1 // P
SLOT = 256
ST = SLOT // P
NSLOT = T // SLOT + E1 - 1
CHUNK = 32
NL = M + E1
VS = D + E0
EPS = 1e-5
B_FIRST = 2
KB = 1024


def build(nc, a, out):
    base = (nc.sbuf_base + 31) // 32 * 32

    class Region:

        def __init__(self, start):
            self.at = start

        def __call__(self, name, shape, dtype):
            t = nc.alloc_sbuf_tensor_at(name, shape, dtype, offset=self.at)
            self.at += (int(np.prod(shape[1:])) * 4 + 31) // 32 * 32
            return t

    def sem(name):
        return nc.alloc_semaphore(name)

    keep = Region(base)
    ident = keep("ident", [P, P], F32)
    tri = keep("tri", [P, P], F32)
    ones = keep("ones", [P, P], F32)
    maskT = keep("maskT", [P, P], F32)
    scan_bias = keep("scan_bias", [P, 3, MC], F32)
    gate_bias = keep("gate_bias", [P, JT, NL], F32)
    ebias = keep("ebias", [P, E1], F32)
    logits = keep("logits", [P, TILES, NL], F32)
    gw_h = keep("gw_h", [P, DC, NL], F32R)
    gw_l = keep("gw_l", [P, DC, NL], F32R)
    gw_raw = keep("gw_raw", [P, DC, NL], F32)
    hstate = keep("hstate", [P, MC], F32)
    neg_half = keep("neg_half", [P, JT], F32)
    pos_i = keep("pos_i", [P, TILES], I32)
    slot_e = keep("slot_e", [P, NSLOT + 1], I32)
    zeros = keep("zeros", [P, D], F32)
    decay = keep("decay", [P, 6], F32)
    WB_h = [[None] * 3 for _ in range(M)]
    WB_l = [[None] * 3 for _ in range(M)]
    for m in range(2):
        for w in range(3):
            WB_h[m][w] = keep(f"WB_h{m}{w}", [P, DC, D], F32R)
            WB_l[m][w] = keep(f"WB_l{m}{w}", [P, DC, D], F32R)
    start_a = keep.at

    ra = Region(start_a)
    x_in = ra("x_in", [P, JT, D], F32)
    xn = ra("xn", [P, JT, D], F32)
    xT_h = ra("xT_h", [P, DC, GT], F32R)
    xT_l = ra("xT_l", [P, DC, GT], F32R)
    at_q = ra.at
    qT = ra("qT", [P, DC, GT], F32)
    kT = ra("kT", [P, DC, GT], F32)
    oT_h = ra("oT_h", [P, DC, GT], F32R)
    oT_l = ra("oT_l", [P, DC, GT], F32R)
    nT_h = ra("nT_h", [P, DC, GT], F32R)
    nT_l = ra("nT_l", [P, DC, GT], F32R)
    sig_g = ra("sig_g", [P, DC, GT], F32)
    v32 = ra("v32", [P, JT, D], F32)
    s32 = ra("s32", [P, JT, P], F32)
    sel = ra("sel", [P, JT, E0], F32)
    hT_h = ra("hT_h", [P, 2, GT], F32R)
    hT_l = ra("hT_l", [P, 2, GT], F32R)
    acc = ra("acc", [P, JT, D], F32)
    x1 = ra("x1", [P, JT, D], F32)
    xn1 = ra("xn1", [P, JT, D], F32)
    ytmp = ra("ytmp", [P, 2, 2, D], F32)
    otmp = ra("otmp", [P, 2, D], F32)
    stats0 = ra("stats0", [P, JT, 6], F32)
    mv0 = ra("mv0", [P, JT, 2], F32)
    rstd0 = ra("rstd0", [P, JT], F32)
    stats1 = ra("stats1", [P, JT, 6], F32)
    mv1 = ra("mv1", [P, JT, 2], F32)
    rstd1 = ra("rstd1", [P, JT], F32)
    stage = ra("stage", [P, 2, 4 * D], F32)
    PW = {}
    for n in ("q", "k", "g", "v", "o"):
        cols = VS if n == "v" else D
        PW[n] = (ra(f"w{n}_h", [P, DC, cols], F32R), ra(f"w{n}_l", [P, DC, cols], F32R))
    keys_h = ra("keys_h", [P, DC, E0 * H0], F32R)
    keys_l = ra("keys_l", [P, DC, E0 * H0], F32R)
    vals_h = ra("vals_h", [P, E0, D], F32R)
    vals_l = ra("vals_l", [P, E0, D], F32R)
    end_a = ra.at

    rb = Region(start_a)
    x1T = rb("x1T", [P, 2, 2, DC, GT], F32R)
    stage_b = rb("stage_b", [P, 2, 4 * D], F32)
    for m in range(2, M):
        for w in range(3):
            WB_h[m][w] = rb(f"WB_h{m}{w}", [P, DC, D], F32R)
            WB_l[m][w] = rb(f"WB_l{m}{w}", [P, DC, D], F32R)
    comb_b = rb("comb_b", [P, 2, M, GT], F32)
    x1_b = rb("x1_b", [P, JT, D], F32)
    y_b = rb("y_b", [P, JT, D], F32)
    res = rb("res", [P, JT, D], F32)
    first_res = rb("first_res", [P, JT, D], F32)
    accT = rb("accT", [P, DC, GT], F32)
    accO = rb("accO", [P, DC, GT], F32)
    idx4 = rb("idx4", [P, JT], I32)
    at_bc = rb.at
    act_o = rb("act_o", [P, 2, 3, GT], F32)
    a_b = rb("a_b", [P, 2, GT], F32)
    xs_b = rb("xs_b", [P, 2, GT], F32)
    h_b = rb("h_b", [P, 2, GT], F32)
    hw_b = rb("hw_b", [P, 2, GT], F32)
    rc = Region(at_bc)
    t32 = rc("t32", [P, FJ, SLOT], F32)
    eT_h = rc("eT_h", [P, FJ, SLOT], F32R)
    eT_l = rc("eT_l", [P, FJ, SLOT], F32R)
    rc.at = max(rc.at, rb.at)
    at_raw = rc.at
    raw1 = rc("raw1", [P, DC, F1], F32)
    raw2 = rc("raw2", [P, FJ, D], F32)
    rows = rc("rows", [P, ST, D], F32)
    sT_h = rc("sT_h", [P, DC, SLOT], F32R)
    sT_l = rc("sT_l", [P, DC, SLOT], F32R)
    y_sb = rc("y_sb", [P, ST, D], F32)
    y0 = nc.alloc_sbuf_tensor_at("y0", [P, JT, D], F32, offset=(at_bc + 31) // 32 * 32 + 40 * KB)
    b1c = rc("b1c", [P, FJ], F32)
    b2b = rc("b2b", [P, D], F32)
    at_w = rc.at
    w1_h = rc("w1_h", [P, DC, F1], F32R)
    w1_l = rc("w1_l", [P, DC, F1], F32R)
    w2_h = rc("w2_h", [P, FJ, D], F32R)
    w2_l = rc("w2_l", [P, FJ, D], F32R)
    rx = Region(at_w)
    xn1_all = rx("xn1_all", [P, TILES, D], F32)
    rr = Region(at_raw)
    rank = rr("rank", [P, TILES, M], F32)
    cmp4 = rr("cmp4", [P, TILES, M], F32)
    top = rr("top", [P, 4, TILES], F32)
    combm = rr("combm", [P, M, TILES], F32)
    combT = rr("combT", [P, P], F32)
    el = rr("el", [P, TILES, E1], F32)
    onehot = rr("onehot", [P, TILES, E1], F32)
    rt1 = rr("rt1", [P, TILES, E1], F32)
    w8 = rr("w8", [P, E1], F32)
    tot = rr("tot", [P, E1, TILES], F32)
    incl = rr("incl", [P, E1, TILES], F32)
    rmax = rr("rmax", [P, TILES], F32)
    k256 = rr("k256", [P, T // SLOT], F32)
    cnt16 = rr("cnt16", [P, E1, T // SLOT], F32)
    nsl = rr("nsl", [P, E1], F32)
    ends = rr("ends", [P, E1], F32)
    s_io = rr("s_io", [P, NSLOT + 1], F32)
    cse = rr("cse", [P, NSLOT + 1, E1], F32)
    sef = rr("sef", [P, NSLOT + 1], F32)
    assert rr.at - at_raw <= 16 * KB and max(end_a, rc.at, rx.at) <= nc.sbuf_usable_end

    rm = Region(at_q)
    diff_i = rm("diff_i", [P, P], I32)
    bit_i = rm("bit_i", [P, P], I32)
    bit_f = rm("bit_f", [P, P], F32)
    nbit_f = rm("nbit_f", [P, P], F32)

    ps = nc.alloc_psum_tensor("ps", [P, 8, 512], F32)
    side2 = ps[:, 6:8, :]
    side4 = ps[:, 6:8, :].rearrange("p b (j d) -> p (b j) d", j=2)

    def yb(k, j):
        return ps[:, 2 + 2 * (k % 2) + j // 2, (j % 2) * D:(j % 2 + 1) * D]

    x1_d = nc.dram_tensor("x1_d", (GROUPS, P, JT, D), F32, kind="Internal").ap()
    xn1_d = nc.dram_tensor("xn1_d", (GROUPS, P, JT, D), F32, kind="Internal").ap()
    xT1_d = nc.dram_tensor("xT1_d", (GROUPS, 2, P, DC, GT), F32, kind="Internal").ap()
    comb_d = nc.dram_tensor("comb_d", (M, T), F32, kind="Internal").ap()
    xs_d = nc.dram_tensor("xs_d", (NSLOT * SLOT, D), F32, kind="Internal").ap()
    y_d = nc.dram_tensor("y_d", (NSLOT * SLOT, D), F32, kind="Internal").ap()

    x_v = a["x"][0].rearrange("(g j p) d -> g p j d", p=P, j=JT)
    out_v = out[0].rearrange("(g j p) d -> g p j d", p=P, j=JT)
    xs_v = xs_d.rearrange("(s i p) d -> s p i d", p=P, i=ST)
    y_v = y_d.rearrange("(s i p) d -> s p i d", p=P, i=ST)

    def cpo(w):
        return w.rearrange("(c p) o -> p c o", p=P)

    chunks = {}
    order = []

    def add_chunk(name, src, hi, lo):
        chunks[name] = (len(order), src, hi, lo)
        order.append(name)

    keys_v = cpo(a["keys"])
    vals_v = a["values"].rearrange("e h v -> h e v")
    for n in ("v", "keys0", "vals0", "q", "k", "g", "keys1", "vals1", "o", "keys2", "vals2", "keys3", "vals3"):
        if n.startswith("keys"):
            s = slice(int(n[4]) * 512, int(n[4]) * 512 + 512)
            add_chunk(n, keys_v[:, :, s], keys_h[:, :, s], keys_l[:, :, s])
        elif n.startswith("vals"):
            s = slice(int(n[4]) * 4, int(n[4]) * 4 + 4)
            add_chunk(n, vals_v[:, s, :], vals_h[:, s, :], vals_l[:, s, :])
        else:
            add_chunk(n, cpo(a["w" + n]), PW[n][0][:], PW[n][1][:])
    for m in range(M):
        for w in range(3):
            add_chunk(f"b{m}{w}", cpo(a["wgvd"][w, m]), WB_h[m][w][:], WB_l[m][w][:])
    n_a_chunks = 13

    def staged(name):
        n, src, hi, _ = chunks[name]
        buf = stage if n < n_a_chunks + 6 else stage_b
        d1, d2 = src.shape[1], src.shape[2]
        return buf[:, n % 2, 0:d1 * d2].rearrange("p (a b) -> p a b", a=d1)

    w_in = [sem("w_in0"), sem("w_in1")]
    w_hi, w_lo = sem("w_hi"), sem("w_lo")
    small_in = sem("small_in")
    consts = sem("consts")
    gw_ready = sem("gw_ready")
    mask_p, mask_v = sem("mask_p"), sem("mask_v")
    dec_s = sem("dec_s")
    setup_v = sem("setup_v")
    ticks = sem("ticks")
    z_out = sem("z_out")
    x_ld = sem("x_ld")
    bn0, mvs0, rs0, xn0 = sem("bn0"), sem("mvs0"), sem("rs0"), sem("xn0")
    bn1, mvs1, rs1, xn1s = sem("bn1"), sem("mvs1"), sem("rs1"), sem("xn1s")
    pe0, pe1 = sem("pe0"), sem("pe1")
    acc_iv, acc_ip = sem("acc_iv"), sem("acc_ip")
    side_full, side_hi, side_free = sem("side_full"), sem("side_hi"), sem("side_free")
    sel_ok = sem("sel_ok")
    s_mask = sem("s_mask")
    o_gate, o_hi, o_23, sg_ok = sem("o_gate"), sem("o_hi"), sem("o_23"), sem("sg_ok")
    h_full, h_hi, h_lo = sem("h_full"), sem("h_hi"), sem("h_lo")
    y_f01, y_f23 = sem("y_f01"), sem("y_f23")
    acc01, y_23, acc23 = sem("acc01"), sem("y_23"), sem("acc23")
    x1_st, xn1_st, xT1_st = sem("x1_st"), sem("xn1_st"), sem("xT1_st")

    N01 = 2 * E0 + 1
    N23 = E0 + 1
    O_STEP = 10

    USES = ["v01", "v23", "q", "k", "g", "s", "t1", "lg", "o", "op", "t0", "t0b"]
    HI_USES = ["t1", "t0", "t0b"]

    def use(g, name, first=False):
        names = [u for u in USES if not (first and u in ("t1", "lg"))]
        start = 2 if first else 12 * g
        return start + names.index(name)

    def hi_use(g, name, first=False):
        names = [u for u in HI_USES if not (first and u == "t1")]
        start = 2 if first else 3 * g + 1
        return start + names.index(name)

    def freed(g, name, first=False):
        names = [u for u in USES if u != "op" and not (first and u in ("t1", "lg"))]
        start = 2 if first else 11 * g
        return start + names.index(name) + 1

    def post_use(g, name):
        if isinstance(g, int) and g == GROUPS - 1:
            n = 1 + (name == "lg")
            return use(g, "op") + n, hi_use(g, "t1") + n, freed(g, "o") + n
        return use(g + 1, name), hi_use(g + 1, "t1"), freed(g + 1, name)

    def wait_alone(eng, s, value):
        eng.wait_ge(s, value)
        eng.sem_inc(ticks, 1)

    def mm3(pe, dst, wh, wl, xh, xl, start, stop):
        pe.matmul(dst, wh, xh, start=start, stop=False)
        pe.matmul(dst, wh, xl, start=False, stop=False)
        return pe.matmul(dst, wl, xh, start=False, stop=stop)

    block = nc.Block("A")
    with block:
        FIRST_SPLITS = {0: ["k"], 1: ["g", "keys1"], 2: ["vals1"], 3: ["o"], 4: ["keys2"], 5: ["vals2"],
                        7: ["keys3"], 8: ["vals3"]}
        LAST_SPLITS = {2: ["b00"], 4: ["b01"], 6: ["b02"], 8: ["b10"], 10: ["b11"], 12: ["b12"]}
        PRO_SPLITS = ["v", "keys0", "vals0", "q"]

        @block.sync
        def _(sp):
            sp.dma_start(x_in[:], x_v[0]).then_inc(x_ld, 16)
            sp.sem_inc(xn1_st, 1)
            sp.sem_inc(xT1_st, 1)

            def weight(name):
                n, src, _, _ = chunks[name]
                if n >= 2:
                    sp.wait_ge(w_lo, n - 1)
                sp.dma_start(staged(name), src).then_inc(w_in[n % 2], 16)

            def body(g, first, last):
                if not last:
                    wait_alone(sp, acc_iv, g + 1)
                    wait_alone(sp, acc_ip, g + 1)
                    sp.dma_start(x_in[:], x_v[g + 1]).then_inc(x_ld, 16)
                if not first:
                    stores(g - 1)

            def stores(g):
                wait_alone(sp, acc01, N01 * (g + 1))
                wait_alone(sp, acc23, N23 * (g + 1))
                sp.dma_start(x1_d[g], x1[:]).then_inc(x1_st, 16)
                wait_alone(sp, xn1s, JT * (g + 1))
                sp.dma_start(xn1_d[g], xn1[:]).then_inc(xn1_st, 16)
                wait_alone(sp, side_free, post_use(g, "t1")[2])
                sp.dma_start(xT1_d[g, 0], nT_h[:].bitcast(F32)).then_inc(xT1_st, 16)
                sp.dma_start(xT1_d[g, 1], nT_l[:].bitcast(F32)).then_inc(xT1_st, 16)

            for name in order[:n_a_chunks]:
                if name == "g":
                    body(0, True, False)
                weight(name)
            with sp.Fori(1, GROUPS - 1) as g:
                body(g, False, False)
            for name in order[n_a_chunks:n_a_chunks + 6]:
                weight(name)
            body(GROUPS - 1, False, True)
            stores(GROUPS - 1)
            sp.wait_ge(x1_st, 16 * GROUPS)
            sp.wait_ge(xn1_st, 1 + 16 * GROUPS)
            sp.wait_ge(xT1_st, 1 + 32 * GROUPS)
            sp.wait_ge(z_out, 16)

        @block.gpsimd
        def _(pool):
            pool.memset(ident[:], 0.0).then_inc(consts, 1)
            pool.memset(ones[:], 1.0).then_inc(consts, 1)
            pool.memset(tri[:], 1.0).then_inc(consts, 1)
            pool.memset(zeros[:], 0.0).then_inc(consts, 1)
            pool.memset(neg_half[:], -0.5).then_inc(consts, 1)
            pool.memset(hstate[:], 0.0).then_inc(consts, 1)
            pool.memset(gate_bias[:], 0.0).then_inc(consts, 1)
            pool.wait_ge(consts, 7)
            pool.affine_select(out=ident[:], in_=ident[:], compare_op=ALU.not_equal, fill=1.0, base=0,
                               pattern=[[-1, P]], channel_multiplier=1).then_inc(consts, 1)
            pool.affine_select(out=tri[:], in_=tri[:], compare_op=ALU.is_gt, fill=0.0, base=0,
                               pattern=[[1, P]], channel_multiplier=-1).then_inc(consts, 1)
            pool.iota(diff_i[:], pattern=[[1, P]], base=0, channel_multiplier=-1).then_inc(consts, 1)

            def rstd(mv, veps, rs, mvs, pes, rss, g):
                wait_alone(pool, mvs, JT * (g + 1))
                pool.tensor_scalar(out=veps, in0=mv[:, :, 1], scalar1=EPS, scalar2=1.0, op0=ALU.add,
                                   op1=ALU.mult).then_inc(pes, 1)
                pool.wait_ge(pes, g + 1)
                pool.tensor_tensor(rs[:], veps, neg_half[:], ALU.pow).then_inc(rss, 1)

            rstd(mv0, stats0[:, :, 0], rstd0, mvs0, pe0, rs0, 0)
            pool.wait_ge(mask_v, 1)
            pool.affine_select(out=maskT[:], in_=maskT[:], compare_op=ALU.is_ge, fill=0.0, base=0,
                               pattern=[[1, P]], channel_multiplier=-1).then_inc(mask_p, 1)
            blocks = maskT[:].rearrange("p (b c) -> p b c", c=CHUNK)
            pool.wait_ge(mask_p, 1)
            pool.affine_select(out=blocks, in_=blocks, compare_op=ALU.is_ge, fill=0.0, base=0,
                               pattern=[[-CHUNK, P // CHUNK], [0, CHUNK]], channel_multiplier=1).then_inc(mask_p, 1)
            pool.wait_ge(mask_p, 2)
            pool.affine_select(out=blocks, in_=blocks, compare_op=ALU.is_ge, fill=0.0, base=CHUNK - 1,
                               pattern=[[CHUNK, P // CHUNK], [0, CHUNK]], channel_multiplier=-1).then_inc(mask_p, 1)

            def body(g, first, last):
                if not first:
                    pool.wait_ge(acc23, N23 * g)
                pool.wait_ge(xn0, JT * (g + 1))
                pool.tensor_tensor(acc[:, 2:4, :], x_in[:, 2:4, :], xn[:, 2:4, :], ALU.add).then_inc(acc_ip, 1)
                pool.wait_ge(acc_ip, g + 1)
                n = 0
                for k in range(E0):
                    pool.wait_ge(y_23, 2 * (E0 * g + k + 1))
                    pool.wait_ge(acc23, N23 * g + n)
                    if k == E0 - 1 and not first:
                        pool.wait_ge(x1_st, 16 * g)
                    dst = x1 if k == E0 - 1 else acc
                    pool.tensor_tensor(dst[:, 2:4, :], acc[:, 2:4, :], ytmp[:, k % 2, :, :], ALU.add).then_inc(acc23, 1)
                    n += 1
                    if k == 1 and not first:
                        rstd(mv1, stats1[:, :, 0], rstd1, mvs1, pe1, rs1, g - 1)
                    if k == 7 and not last:
                        rstd(mv0, stats0[:, :, 0], rstd0, mvs0, pe0, rs0, g + 1)
                    if k == O_STEP:
                        pool.wait_ge(o_23, g + 1)
                        pool.wait_ge(acc23, N23 * g + n)
                        pool.tensor_tensor(acc[:, 2:4, :], acc[:, 2:4, :], otmp[:], ALU.add).then_inc(acc23, 1)
                        n += 1

            body(0, True, False)
            with pool.Fori(1, GROUPS - 1) as g:
                body(g, False, False)
            body(GROUPS - 1, False, True)
            rstd(mv1, stats1[:, :, 0], rstd1, mvs1, pe1, rs1, GROUPS - 1)

        @block.scalar
        def _(act):
            act.dma_start(decay[:, 5:6], a["log_decay"][0:1].rearrange("(o n) -> o n", o=1).to_broadcast((P, 1))).then_inc(small_in, 16)
            act.dma_start(gw_raw[:], cpo(a["gates"])).then_inc(small_in, 16)
            act.dma_start(scan_bias[:], a["scan_bias"]).then_inc(small_in, 16)
            act.dma_start(ebias[:], a["expert_bias"].rearrange("(o n) -> o n", o=1).to_broadcast((P, E1))).then_inc(small_in, 16)
            act.wait_ge(consts, 7)
            for j in range(JT):
                act.dma_start(gate_bias[:, j, M:NL], a["gate_b"].rearrange("(o n) -> o n", o=1).to_broadcast((P, E1))).then_inc(small_in, 16)
            act.dma_start(xs_d.rearrange("(r p) d -> p r d", p=P),
                          zeros[:].unsqueeze(1).to_broadcast((P, NSLOT * ST, D))).then_inc(z_out, 16)
            act.wait_ge(small_in, 16 * (4 + JT))
            act.activation(decay[:, 0:1], decay[:, 5:6], ACT.Sigmoid).then_inc(dec_s, 1)
            act.activation(gw_h[:], gw_raw[:], ACT.Copy).then_inc(gw_ready, 1)

            def split(name):
                n, _, hi, _ = chunks[name]
                act.wait_ge(w_in[n % 2], 16 * (n // 2 + 1))
                act.activation(hi, staged(name), ACT.Copy).then_inc(w_hi, 1)

            def relu_hi(g, k, first):
                act.wait_ge(h_full, E0 * g + k + 1)
                if not (first and k < 2):
                    act.wait_ge(y_f23, E0 * g + k - 1)
                act.activation(hT_h[:, k % 2, :], ps[:, k % 2, :], ACT.Relu).then_inc(h_hi, 1)

            def t_hi(n, dst, src):
                act.wait_ge(side_full, n + 1)
                act.activation(dst, src, ACT.Copy).then_inc(side_hi, 1)

            def xT_parts(g, name, first):
                for c in range(DC):
                    t_hi(use(g, name, first) + c, xT_h[:, c, :], ps[:, 6 + c, :])

            def values(g, half, first):
                n = use(g, "v01" if half == 0 else "v23", first)
                act.wait_ge(side_full, n + 1)
                act.activation(sel[:, 2 * half:2 * half + 2, :], side2[:, :, D:VS], ACT.Sigmoid).then_inc(sel_ok, 1)
                act.activation(v32[:, 2 * half:2 * half + 2, :], side2[:, :, 0:D], ACT.Copy).then_inc(side_free, 1)

            def body(g, first, last):
                if first:
                    splits = FIRST_SPLITS
                else:
                    splits = LAST_SPLITS if last else {}
                relu_hi(g, 0, first)
                if not first:
                    act.wait_ge(acc01, N01 * g)
                values(g, 0, first)
                relu_hi(g, 1, first)
                values(g, 1, first)
                for k in range(E0):
                    if 1 <= k < E0 - 1:
                        relu_hi(g, k + 1, first)
                    if k == E0 - 2 and not last:
                        xT_parts(g, "t0", first)
                    act.wait_ge(y_f23, E0 * g + k + 1)
                    if not (first and k < 2):
                        act.wait_ge(acc23, N23 * g + k - 1 + (1 if k - 2 >= O_STEP else 0))
                    if k == 0:
                        act.wait_ge(sel_ok, 2 * (g + 1))
                    for j in (2, 3):
                        act.activation(ytmp[:, k % 2, j - 2, :], yb(k, j), ACT.Copy,
                                       scale=sel[:, j, k:k + 1]).then_inc(y_23, 1)
                    if k == 2:
                        act.wait_ge(side_full, use(g, "k", first) + 1)
                        act.activation(kT[:], side2, ACT.Copy).then_inc(side_free, 1)
                    if k == 3:
                        act.wait_ge(side_full, use(g, "g", first) + 1)
                        act.activation(sig_g[:], side2, ACT.Sigmoid).then_inc(side_free, 1)
                    if k == 5 and not first:
                        act.wait_ge(xT1_st, 1 + 32 * (g - 1))
                        t_hi(use(g, "t1"), nT_h[:], side2)
                    if k == 7:
                        act.wait_ge(o_gate, g + 1)
                        act.activation(oT_h[:], sig_g[:], ACT.Copy).then_inc(o_hi, 1)
                    if k == O_STEP:
                        act.wait_ge(side_full, use(g, "op", first) + 1)
                        if not first:
                            act.wait_ge(acc23, N23 * (g - 1) + O_STEP + 2)
                        act.activation(otmp[:], side4[:, 2:4, :], ACT.Copy).then_inc(o_23, 1)
                    for name in splits.get(k, []):
                        split(name)

            split("v")
            for c in range(DC):
                t_hi(c, xT_h[:, c, :], ps[:, 6 + c, :])
            for name in PRO_SPLITS[1:]:
                split(name)
            body(0, True, False)
            with act.Fori(1, GROUPS - 1) as g:
                body(g, False, False)
            body(GROUPS - 1, False, True)
            act.wait_ge(xT1_st, 1 + 32 * (GROUPS - 1))
            t_hi(post_use(GROUPS - 1, "t1")[0], nT_h[:], side2)

        @block.vector
        def _(dve):
            made = [0]

            def setup(ins):
                made[0] += 1
                ins.then_inc(setup_v, 1)
                dve.wait_ge(setup_v, made[0])

            def split(name):
                n, _, hi, lo = chunks[name]
                dve.wait_ge(w_hi, n + 1)
                dve.tensor_tensor(lo, staged(name), hi.bitcast(F32), ALU.subtract).then_inc(w_lo, 1)

            def ln_stats(x, st, bn, tiles=range(JT)):
                for j in tiles:
                    dve.bn_stats(st[:, j, :], x[:, j, :]).then_inc(bn, 1)

            def ln_aggr(st, mv, bn, mvs, g):
                wait_alone(dve, bn, JT * (g + 1))
                for j in range(JT):
                    dve.bn_aggr(mv[:, j, :], st[:, j, :]).then_inc(mvs, 1)

            def ln_norm(dst, x, mv, rs, rss, done, g, tiles=range(JT)):
                dve.wait_ge(rss, g + 1)
                for j in tiles:
                    dve.tensor_scalar(out=dst[:, j, :], in0=x[:, j, :], scalar1=mv[:, j, 0:1],
                                      scalar2=rs[:, j:j + 1], op0=ALU.subtract, op1=ALU.mult).then_inc(done, 1)

            def lo_of(nh, dst, hi, src):
                dve.wait_ge(side_hi, nh + 1)
                dve.tensor_tensor(dst, src, hi.bitcast(F32), ALU.subtract).then_inc(side_free, 1)

            def xT_lo(nh):
                for c in range(DC):
                    lo_of(nh + c, xT_l[:, c, :], xT_h[:, c, :], ps[:, 6 + c, :])

            def relu_lo(g, k):
                dve.wait_ge(h_hi, E0 * g + k + 1)
                dve.scalar_tensor_tensor(out=hT_l[:, k % 2, :], in0=ps[:, k % 2, :], scalar=0.0,
                                         in1=hT_h[:, k % 2, :].bitcast(F32), op0=ALU.max,
                                         op1=ALU.subtract).then_inc(h_lo, 1)

            def body(g, first, last):
                if first:
                    splits = FIRST_SPLITS
                else:
                    splits = LAST_SPLITS if last else {}
                relu_lo(g, 0)
                relu_lo(g, 1)
                dve.wait_ge(xn0, JT * (g + 1))
                dve.tensor_tensor(acc[:, 0:2, :], x_in[:, 0:2, :], xn[:, 0:2, :], ALU.add).then_inc(acc_iv, 1)
                dve.wait_ge(sel_ok, 2 * g + 2)
                dve.wait_ge(acc_iv, g + 1)
                n = 0
                for k in range(E0):
                    if 1 <= k < E0 - 1:
                        relu_lo(g, k + 1)
                    if k == E0 - 2 and not last:
                        xT_lo(hi_use(g, "t0", first))
                    dve.wait_ge(y_f01, E0 * g + k + 1)
                    if k == E0 - 1 and not first:
                        dve.wait_ge(x1_st, 16 * g)
                    dst = x1 if k == E0 - 1 else acc
                    if k > 0:
                        dve.wait_ge(acc01, N01 * g + n)
                    for j in (0, 1):
                        dve.scalar_tensor_tensor(out=dst[:, j, :], in0=yb(k, j), scalar=sel[:, j, k:k + 1],
                                                 in1=acc[:, j, :], op0=ALU.mult, op1=ALU.add).then_inc(acc01, 1)
                        n += 1
                    if k == 1:
                        dve.wait_ge(side_full, use(g, "q", first) + 1)
                        dve.tensor_copy(qT[:], side2).then_inc(side_free, 1)
                    if k == 0 and not first:
                        ln1_stats(g - 1, range(0, 2))
                    if k == 1 and not first:
                        ln1_stats(g - 1, range(2, 4))
                        ln_aggr(stats1, mv1, bn1, mvs1, g - 1)
                    if k == 3 and not first:
                        ln1_norm(g - 1, range(0, 2))
                    if k == 4 and not first:
                        ln1_norm(g - 1, range(2, 4))
                    if k == 4:
                        dve.wait_ge(side_full, use(g, "s", first) + 1)
                        if first:
                            dve.wait_ge(mask_p, 3)
                        dve.tensor_tensor(s32[:], ps[:, 6, :].rearrange("p (j c) -> p j c", j=JT),
                                          maskT[:].unsqueeze(1).to_broadcast((P, JT, P)), ALU.mult).then_inc(side_free, 1)
                    if k == 5 and not first:
                        lo_of(hi_use(g, "t1"), nT_l[:], nT_h[:], side2)
                    if k == 6 and not first:
                        gate_logits(g - 1)
                    if k == 7:
                        dve.wait_ge(side_full, use(g, "o", first) + 1)
                        dve.tensor_tensor(sig_g[:], side2, sig_g[:], ALU.mult).then_inc(o_gate, 1)
                    if k == 8:
                        dve.wait_ge(o_hi, g + 1)
                        dve.tensor_tensor(oT_l[:], sig_g[:], oT_h[:].bitcast(F32), ALU.subtract).then_inc(side_free, 1)
                    if k == 5 and not last:
                        dve.wait_ge(x_ld, 16 * (g + 2))
                        ln_stats(x_in, stats0, bn0, range(0, 2))
                    if k == 6 and not last:
                        ln_stats(x_in, stats0, bn0, range(2, 4))
                    if k == 7 and not last:
                        ln_aggr(stats0, mv0, bn0, mvs0, g + 1)
                    if k in (9, 11) and not last:
                        if k == 9:
                            dve.wait_ge(acc_ip, g + 1)
                        ln_norm(xn, x_in, mv0, rstd0, rs0, xn0, g + 1, range(k - 9, k - 7))
                    if k == O_STEP:
                        dve.wait_ge(side_full, use(g, "op", first) + 1)
                        dve.wait_ge(acc01, N01 * g + n)
                        dve.tensor_tensor(acc[:, 0:2, :], side4[:, 0:2, :], acc[:, 0:2, :], ALU.add).then_inc(acc01, 1)
                        n += 1
                    for name in splits.get(k, []):
                        split(name)

            def ln1_stats(g, tiles):
                if 0 in tiles:
                    dve.wait_ge(acc01, N01 * (g + 1))
                else:
                    dve.wait_ge(acc23, N23 * (g + 1))
                ln_stats(x1, stats1, bn1, tiles)

            def ln1_norm(g, tiles):
                dve.wait_ge(xn1_st, 1 + 16 * g)
                ln_norm(xn1, x1, mv1, rstd1, rs1, xn1s, g, tiles)

            def gate_logits(g):
                dve.wait_ge(side_full, post_use(g, "lg")[0] + 1)
                dve.tensor_tensor(logits[:, bass.ds(g * JT, JT), :], ps[:, 6, 0:JT * NL].rearrange("p (j n) -> p j n", j=JT),
                                  gate_bias[:], ALU.add).then_inc(side_free, 1)

            dve.wait_ge(x_ld, 16)
            ln_stats(x_in, stats0, bn0)
            ln_aggr(stats0, mv0, bn0, mvs0, 0)
            ln_norm(xn, x_in, mv0, rstd0, rs0, xn0, 0)
            split("v")
            xT_lo(0)
            dve.wait_ge(dec_s, 1)
            for b in range(1, 5):
                setup(dve.tensor_tensor(decay[:, b:b + 1], decay[:, b - 1:b], decay[:, b - 1:b], ALU.mult))
            dve.wait_ge(consts, 10)
            for b in range(5):
                setup(dve.tensor_scalar(out=bit_i[:], in0=diff_i[:], scalar1=b, scalar2=1, op0=ALU.arith_shift_right,
                                        op1=ALU.bitwise_and))
                setup(dve.tensor_copy(bit_f[:], bit_i[:]))
                setup(dve.tensor_scalar(out=nbit_f[:], in0=bit_f[:], scalar1=-1.0, scalar2=1.0, op0=ALU.mult,
                                        op1=ALU.add))
                power = maskT if b == 0 else bit_f
                setup(dve.scalar_tensor_tensor(out=power[:], in0=bit_f[:], scalar=decay[:, b:b + 1], in1=nbit_f[:],
                                               op0=ALU.mult, op1=ALU.add))
                if b:
                    setup(dve.tensor_tensor(maskT[:], maskT[:], bit_f[:], ALU.mult))
            dve.engine_nop().then_inc(mask_v, 1)
            dve.wait_ge(gw_ready, 1)
            dve.tensor_tensor(gw_l[:], gw_raw[:], gw_h[:].bitcast(F32), ALU.subtract).then_inc(gw_ready, 1)
            for name in PRO_SPLITS[1:]:
                split(name)
            body(0, True, False)
            with dve.Fori(1, GROUPS - 1) as g:
                body(g, False, False)
            body(GROUPS - 1, False, True)
            g = GROUPS - 1
            for tiles in (range(0, 2), range(2, 4)):
                ln1_stats(g, tiles)
            ln_aggr(stats1, mv1, bn1, mvs1, g)
            ln1_norm(g, range(JT))
            lo_of(post_use(g, "t1")[1], nT_l[:], nT_h[:], side2)
            gate_logits(g)

        @block.tensor
        def _(pe):
            def transposes(src, n):
                for c in range(DC):
                    for j in range(JT):
                        last = pe.transpose(side2[:, c, j * P:(j + 1) * P], src[:, j, c * P:(c + 1) * P], ident[:])
                    if n == DC or c == DC - 1:
                        last.then_inc(side_full, 1)

            def body(g, first, last):
                def ready(name):
                    pe.wait_ge(side_free, freed(g, name, first))

                def weights(name):
                    if first:
                        pe.wait_ge(w_lo, chunks[name][0] + 1)

                def up(k):
                    weights(f"keys{k // 4}")
                    if not (first and k < 2):
                        pe.wait_ge(h_lo, E0 * g + k - 1)
                    s = slice(k * H0, (k + 1) * H0)
                    for c in range(DC):
                        last = mm3(pe, ps[:, k % 2, :], keys_h[:, c, s], keys_l[:, c, s], xT_h[:, c, :], xT_l[:, c, :],
                                   c == 0, c == DC - 1)
                    last.then_inc(h_full, 1)

                def down(k):
                    weights(f"vals{k // 4}")
                    pe.wait_ge(h_lo, E0 * g + k + 1)
                    for half, done in ((0, y_f01), (1, y_f23)):
                        if not (first and k < 2):
                            if half == 0:
                                pe.wait_ge(acc01, N01 * g + 2 * (k - 1) + (1 if k - 2 >= O_STEP + 1 else 0))
                            else:
                                pe.wait_ge(y_23, 2 * (E0 * g + k - 1))
                        for j in (2 * half, 2 * half + 1):
                            s = slice(j * P, (j + 1) * P)
                            pe.matmul(yb(k, j), hT_h[:, k % 2, s], vals_h[:, k, :], start=True, stop=False)
                            pe.matmul(yb(k, j), hT_h[:, k % 2, s], vals_l[:, k, :], start=False, stop=False)
                            last_mm = pe.matmul(yb(k, j), hT_l[:, k % 2, s], vals_h[:, k, :], start=False, stop=True)
                        last_mm.then_inc(done, 1)

                def project(n):
                    weights(n)
                    for o in range(DC):
                        for c in range(DC):
                            s = slice(o * P, (o + 1) * P)
                            last_mm = mm3(pe, side2[:, o, :], PW[n][0][:, c, s], PW[n][1][:, c, s], xT_h[:, c, :],
                                          xT_l[:, c, :], c == 0, c == DC - 1)
                    last_mm.then_inc(side_full, 1)

                def rows_times(dst, th, tl, j, wh, wl):
                    s = slice(j * P, (j + 1) * P)
                    for c in range(DC):
                        pe.matmul(dst, th[:, c, s], wh[:, c, :], start=c == 0, stop=False)
                        pe.matmul(dst, th[:, c, s], wl[:, c, :], start=False, stop=False)
                        last_mm = pe.matmul(dst, tl[:, c, s], wh[:, c, :], start=False, stop=c == DC - 1)
                    return last_mm

                def values(half):
                    weights("v")
                    for j in (0, 1):
                        last_mm = rows_times(side2[:, j, 0:VS], xT_h, xT_l, 2 * half + j, *PW["v"])
                    last_mm.then_inc(side_full, 1)

                pe.wait_ge(side_free, 2 if first else freed(g, "v01") - 1)
                up(0)
                values(0)
                up(1)
                ready("v01")
                values(1)
                for k in range(E0):
                    if 1 <= k < E0 - 1:
                        up(k + 1)
                    down(k)
                    if k == 1:
                        ready("v23")
                        project("q")
                    if k == 2:
                        ready("q")
                        project("k")
                    if k == 3:
                        ready("k")
                        project("g")
                    if k == 4:
                        ready("g")
                        for j in range(JT):
                            s = slice(j * P, (j + 1) * P)
                            for c in range(DC):
                                last_mm = pe.matmul(ps[:, 6, s], kT[:, c, s], qT[:, c, s], start=c == 0,
                                                    stop=c == DC - 1)
                        last_mm.then_inc(side_full, 1)
                    if k == 5 and not first:
                        post_transposes(g - 1)
                    if k == 6 and not first:
                        post_logits(g - 1)
                    if k == 7:
                        ready("s" if first else "lg")
                        for c in range(DC):
                            for j in range(JT):
                                last_mm = pe.matmul(side2[:, c, j * P:(j + 1) * P], v32[:, j, c * P:(c + 1) * P],
                                                    s32[:, j, :], start=True, stop=True)
                        last_mm.then_inc(side_full, 1)
                    if k == O_STEP:
                        ready("o")
                        weights("o")
                        for j in range(JT):
                            last_mm = rows_times(side4[:, j, :], oT_h, oT_l, j, *PW["o"])
                        last_mm.then_inc(side_full, 1)
                    if k == E0 - 3 and not last:
                        pe.wait_ge(xn0, JT * (g + 2))
                        pe.wait_ge(o_23, g + 1)
                        pe.wait_ge(acc01, N01 * g + 2 * (O_STEP + 1) + 1)
                        transposes(xn, DC)

            def post_transposes(g):
                pe.wait_ge(xn1s, JT * (g + 1))
                if isinstance(g, int) and g == GROUPS - 1:
                    pe.wait_ge(o_23, g + 1)
                    pe.wait_ge(acc01, N01 * (g + 1))
                else:
                    pe.wait_ge(side_free, freed(g + 1, "s"))
                transposes(xn1, 1)

            def post_logits(g):
                pe.wait_ge(side_free, post_use(g, "t1")[2])
                for j in range(JT):
                    s = slice(j * P, (j + 1) * P)
                    for c in range(DC):
                        pe.matmul(ps[:, 6, j * NL:(j + 1) * NL], nT_h[:, c, s], gw_h[:, c, :], start=c == 0, stop=False)
                        pe.matmul(ps[:, 6, j * NL:(j + 1) * NL], nT_h[:, c, s], gw_l[:, c, :], start=False, stop=False)
                        last_mm = pe.matmul(ps[:, 6, j * NL:(j + 1) * NL], nT_l[:, c, s], gw_h[:, c, :], start=False,
                                            stop=c == DC - 1)
                last_mm.then_inc(side_full, 1)

            pe.wait_ge(consts, 8)
            pe.wait_ge(xn0, JT)
            transposes(xn, DC)
            pe.wait_ge(gw_ready, 2)
            body(0, True, False)
            with pe.Fori(1, GROUPS - 1) as g:
                body(g, False, False)
            body(GROUPS - 1, False, True)
            post_transposes(GROUPS - 1)
            post_logits(GROUPS - 1)


    wb_lo = sem("wb_lo")
    wb_hi = sem("wb_hi")
    wb_in = [sem("wb_in0"), sem("wb_in1")]
    xn_in = sem("xn_in")
    x1T_in, comb_in, x1b_in = sem("x1T_in"), sem("comb_in"), sem("x1b_in")
    b_full, act_g = sem("b_full"), sem("act_g")
    xs_ok, a_ok, scan_ok, hst, hw_ok, acc_ok = (sem(n) for n in ("xs_ok", "a_ok", "scan_ok", "hst", "hw_ok", "acc_ok"))
    fin_full, fin_sum, fin_ok, out_st = (sem(n) for n in ("fin_full", "fin_sum", "fin_ok", "out_st"))
    r_io, r_v, r_top, r_sig, r_comb, r_ct, r_cs, comb_st = (
        sem(n) for n in ("r_io", "r_v", "r_top", "r_sig", "r_comb", "r_ct", "r_cs", "comb_st"))
    r_hot, r_cum, r_pos, r_slot = (sem(n) for n in ("r_hot", "r_cum", "r_pos", "r_slot"))
    scat, idx_ok, y_in, y0_in = sem("scat"), sem("idx_ok"), sem("y_in"), sem("y0_in")
    r1_in, r2_in, b1_in, b2_in, rows_in = (sem(n) for n in ("r1_in", "r2_in", "b1_in", "b2_in", "rows_in"))
    w1_hi, w1_lo, w2_hi, w2_lo = (sem(n) for n in ("w1_hi", "w1_lo", "w2_hi", "w2_lo"))
    T_full, sT_hi, sT_ok = sem("T_full"), sem("sT_hi"), sem("sT_ok")
    l1_full, t_ok, e_hi, e_ok, l2_full, ys_ok, y_st = (
        sem(n) for n in ("l1_full", "t_ok", "e_hi", "e_ok", "l2_full", "ys_ok", "y_st"))

    w1_v = a["w1"].rearrange("e (c p) f -> e p c f", p=P)
    w2_v = a["w2"].rearrange("e (j p) d -> e p j d", p=P)
    HALF1, HALF2 = F1 // 2, FJ // 2
    late = order[n_a_chunks + 6:]

    def zero(g):
        return isinstance(g, int) and g == 0

    def ring(g):
        return g % 2

    with nc.Block("RBC") as block:

        @block.sync
        def _(sp):
            def load_x1T(g):
                if not zero(g):
                    wait_alone(sp, x1T_in, 32 * g)
                if not (isinstance(g, int) and g < 2):
                    wait_alone(sp, b_full, 3 * MC * (g - 1))
                for part in (0, 1):
                    sp.dma_start(x1T[:, bass.ds(ring(g), 1), part, :, :].bitcast(F32),
                                 xT1_d[bass.ds(g, 1), part].rearrange("a p c t -> p a c t")).then_inc(x1T_in, 16)

            def load_comb(g):
                if not zero(g):
                    wait_alone(sp, comb_in, 16 * g)
                if not (isinstance(g, int) and g < 2):
                    wait_alone(sp, hw_ok, MC * (g - 1))
                sp.dma_start(comb_b[:, bass.ds(ring(g), 1), :, :],
                             comb_d[:, bass.ds(g * GT, GT)].rearrange("(o a) t -> o a t", o=1).unsqueeze(0)
                             .to_broadcast((P, 1, M, GT))).then_inc(comb_in, 16)

            def body(g, last=False):
                if not last:
                    load_x1T(g + 1)
                    if not zero(g):
                        load_comb(g + 1)
                if not zero(g):
                    wait_alone(sp, fin_ok, g)
                    if not (isinstance(g, int) and g == 1):
                        sp.dma_start(out_v[bass.ds(g - 1, 1)].rearrange("a p j d -> p (a j) d"), res[:]).then_inc(out_st, 16)
                sp.dma_start(x1_b[:], x1_d[bass.ds(g, 1)].rearrange("a p j d -> p (a j) d")).then_inc(x1b_in, 16)

            def load_late(i):
                if i >= 2:
                    sp.wait_ge(wb_lo, i - 1)
                n, src, _, _ = chunks[late[i]]
                sp.dma_start(staged(late[i]), src).then_inc(wb_in[n % 2], 16)

            load_x1T(0)
            load_late(0)
            load_late(1)
            sp.dma_start(xn1_all[:].rearrange("p (g j) d -> p g j d", j=JT),
                         xn1_d.rearrange("g p j d -> p g j d")).then_inc(xn_in, 16)
            load_late(2)
            load_late(3)
            sp.wait_ge(r_cs, 1)
            sp.dma_start(comb_d.rearrange("m (t p) -> (m t) p", p=P), combT[:]).then_inc(comb_st, 16)
            sp.wait_ge(comb_st, 16)
            load_comb(0)
            load_comb(1)
            load_late(4)
            load_late(5)
            for g in range(B_FIRST):
                body(g)

            def slot(s, first=False):
                if first:
                    sp.wait_ge(r_slot, 1)
                    sp.wait_ge(scat, 16 * TILES)
                else:
                    wait_alone(sp, w1_lo, 2 * s)
                e = sp.value_load(slot_e[0:1, bass.ds(s, 1)], min_val=0, max_val=E1 - 1)
                sp.dma_start(raw1[:], w1_v[bass.ds(e, 1)].rearrange("a p c f -> p (a c) f")).then_inc(r1_in, 16)
                if not first:
                    wait_alone(sp, T_full, s)
                sp.dma_start(rows[:], xs_v[bass.ds(s, 1)].rearrange("a p i d -> p (a i) d")).then_inc(rows_in, 16)
                if not (isinstance(s, int) and s < 2):
                    finish(s - 2)
                if not first:
                    b2_of(s - 1)
                    wait_alone(sp, w2_lo, 2 * s)
                sp.dma_start(raw2[:], w2_v[bass.ds(e, 1)].rearrange("a p j d -> p (a j) d")).then_inc(r2_in, 16)
                if not first:
                    wait_alone(sp, t_ok, FJ * s)
                sp.dma_start(b1c[:], a["b1"][bass.ds(e, 1)].rearrange("a p j -> p (a j)")).then_inc(b1_in, 16)

            def finish(s):
                wait_alone(sp, ys_ok, s + 1)
                sp.dma_start(y_v[bass.ds(s, 1)].rearrange("a p i d -> p (a i) d"), y_sb[:]).then_inc(y_st, 16)

            def b2_of(s):
                e = sp.value_load(slot_e[0:1, bass.ds(s, 1)], min_val=0, max_val=E1 - 1)
                sp.dma_start(b2b[:], a["b2"][bass.ds(e, 1)].to_broadcast((P, D))).then_inc(b2_in, 16)

            slot(0, True)
            slot(1)
            with sp.Fori(2, NSLOT) as s:
                slot(s)
            finish(NSLOT - 2)
            b2_of(NSLOT - 1)
            finish(NSLOT - 1)
            with sp.Fori(B_FIRST, GROUPS - 1) as g:
                body(g)
            body(GROUPS - 1, True)
            sp.wait_ge(fin_ok, GROUPS)
            sp.dma_start(out_v[GROUPS - 1], res[:]).then_inc(out_st, 16)
            sp.wait_ge(fin_ok, GROUPS + 1)
            sp.dma_start(out_v[0], first_res[:]).then_inc(out_st, 16)
            sp.wait_ge(out_st, 16 * GROUPS)

        @block.tensor
        def _(pe):
            def step(g, i):
                m, c = divmod(i, DC)
                if not (zero(g) and i < 2):
                    pe.wait_ge(act_g, 3 * (MC * g + i - 1))
                for w in range(3):
                    if zero(g) and m >= 2:
                        pe.wait_ge(wb_lo, (m - 2) * 3 + w + 1)
                    s = slice(c * P, (c + 1) * P)
                    for k in range(DC):
                        last_mm = mm3(pe, ps[:, 3 * (i % 2) + w, :], WB_h[m][w][:, k, s], WB_l[m][w][:, k, s],
                                      x1T[:, bass.ds(ring(g), 1), 0, k, :], x1T[:, bass.ds(ring(g), 1), 1, k, :],
                                      k == 0, k == DC - 1)
                    last_mm.then_inc(b_full, 1)

            def to_rows(g):
                pe.wait_ge(acc_ok, 6 * (g + 1))
                if not zero(g):
                    pe.wait_ge(fin_ok, g)
                for j in range(JT):
                    for c in range(DC):
                        last_mm = pe.transpose(side4[:, j, c * P:(c + 1) * P], accT[:, c, j * P:(j + 1) * P], ident[:])
                last_mm.then_inc(fin_full, 1)

            def body(g):
                pe.wait_ge(x1T_in, 32 * (g + 1))
                for i in range(MC):
                    step(g, i)
                    if zero(g) and i == 1:
                        pe.wait_ge(r_comb, 1)
                        pe.transpose(ps[:, 6, 0:P], combm[:].rearrange("p m t -> p (m t)"), ident[:]).then_inc(r_ct, 1)
                    if zero(g) and i == 3:
                        pe.wait_ge(r_hot, 1)
                        hot = onehot[:].rearrange("p t e -> p (t e)")
                        pe.matmul(ps[:, 7, 0:256], tri[:], hot, start=True, stop=True)
                        pe.matmul(ps[:, 7, 256:512], ones[:], hot, start=True, stop=True).then_inc(r_cum, 1)
                    if i == 2 and not zero(g):
                        to_rows(g - 1)

            for g in range(B_FIRST):
                body(g)

            def rows_T(s):
                pe.wait_ge(rows_in, 16 * (s + 1))
                if not zero(s):
                    pe.wait_ge(sT_ok, s)
                for c in range(DC):
                    for i in range(ST):
                        last_mm = pe.transpose(ps[:, 6, c * SLOT + i * P:c * SLOT + (i + 1) * P],
                                               rows[:, i, c * P:(c + 1) * P], ident[:])
                last_mm.then_inc(T_full, 1)

            def slot(s, last=False):
                pe.wait_ge(sT_ok, s + 1)
                for q in range(FJ // 2):
                    if not zero(s):
                        pe.wait_ge(t_ok, FJ * (s - 1) + 2 * q + 2)
                    if q in (0, 2):
                        pe.wait_ge(w1_lo, 2 * s + 1 + q // 2)
                    for j in (2 * q, 2 * q + 1):
                        f = slice(j * P, (j + 1) * P)
                        for c in range(DC):
                            last_mm = mm3(pe, ps[:, q, (j % 2) * SLOT:(j % 2 + 1) * SLOT], w1_h[:, c, f], w1_l[:, c, f],
                                          sT_h[:, c, :], sT_l[:, c, :], c == 0, c == DC - 1)
                    last_mm.then_inc(l1_full, 1)
                if not last:
                    rows_T(s + 1)
                if not zero(s):
                    pe.wait_ge(ys_ok, s)
                for j in range(FJ):
                    if j % 2 == 0:
                        pe.wait_ge(e_ok, FJ // 2 * s + j // 2 + 1)
                    if j in (0, HALF2):
                        pe.wait_ge(w2_lo, 2 * s + 1 + j // HALF2)
                    for i in range(ST):
                        r = slice(i * P, (i + 1) * P)
                        dst = ps[:, 4 + i, 0:D]
                        pe.matmul(dst, eT_h[:, j, r], w2_h[:, j, :], start=j == 0, stop=False)
                        pe.matmul(dst, eT_h[:, j, r], w2_l[:, j, :], start=False, stop=False)
                        last_mm = pe.matmul(dst, eT_l[:, j, r], w2_h[:, j, :], start=False, stop=j == FJ - 1)
                last_mm.then_inc(l2_full, 1)

            rows_T(0)
            slot(0)
            with pe.Fori(1, NSLOT - 1) as s:
                slot(s)
            slot(NSLOT - 1, True)
            pe.wait_ge(ys_ok, NSLOT)
            with pe.Fori(B_FIRST, GROUPS) as g:
                body(g)
            to_rows(GROUPS - 1)

        @block.scalar
        def _(act):
            def step(g, i):
                n = MC * g + i
                if not (zero(g) and i < 2):
                    act.wait_ge(xs_ok, n - 1)
                    act.wait_ge(a_ok, n - 1)
                for w, func in enumerate((ACT.Sigmoid, ACT.Tanh, ACT.Sigmoid)):
                    act.wait_ge(b_full, 3 * n + w + 1)
                    act.activation(act_o[:, i % 2, w, :], ps[:, 3 * (i % 2) + w, :], func,
                                   bias=scan_bias[:, w, i:i + 1]).then_inc(act_g, 1)

            def split_late(i):
                name = late[i]
                n = chunks[name][0]
                act.wait_ge(wb_in[n % 2], 16 * (i // 2 + 1))
                act.activation(chunks[name][2], staged(name), ACT.Copy).then_inc(wb_hi, 1)

            for i in range(2):
                split_late(i)
            act.wait_ge(r_top, 1)
            act.activation(top[:, 2, :], top[:, 3, :], ACT.Sigmoid).then_inc(r_sig, 1)
            act.activation(top[:, 1, :], top[:, 3, :], ACT.Sigmoid, scale=-1.0).then_inc(r_sig, 1)
            for g in range(B_FIRST):
                for i in range(MC):
                    step(g, i)
                    if g == 0 and i < 4:
                        split_late(i + 2)
                    if g == 0 and i == 1:
                        act.wait_ge(r_ct, 1)
                        act.activation(combT[:], ps[:, 6, 0:P], ACT.Copy).then_inc(r_cs, 1)

            def w1_half(s, h):
                if h == 0:
                    act.wait_ge(r1_in, 16 * (s + 1))
                if not zero(s):
                    act.wait_ge(l1_full, FJ // 2 * (s - 1) + 2 * (h + 1))
                f = slice(h * HALF1, (h + 1) * HALF1)
                act.activation(w1_h[:, :, f], raw1[:, :, f], ACT.Copy).then_inc(w1_hi, 1)

            def w2_half(s, h):
                if h == 0:
                    act.wait_ge(r2_in, 16 * (s + 1))
                    if not zero(s):
                        act.wait_ge(l2_full, s)
                j = slice(h * HALF2, (h + 1) * HALF2)
                act.activation(w2_h[:, j, :], raw2[:, j, :], ACT.Copy).then_inc(w2_hi, 1)

            def rows_hi(s):
                act.wait_ge(T_full, s + 1)
                act.activation(sT_h[:].rearrange("p c t -> p (c t)"), ps[:, 6, :], ACT.Copy).then_inc(sT_hi, 1)

            def relu(s, q):
                act.wait_ge(l1_full, FJ // 2 * s + q + 1)
                if q == 0:
                    act.wait_ge(b1_in, 16 * (s + 1))
                if not zero(s):
                    act.wait_ge(e_ok, FJ // 2 * (s - 1) + q + 1)
                for j in (2 * q, 2 * q + 1):
                    act.activation(t32[:, j, :], ps[:, q, (j % 2) * SLOT:(j % 2 + 1) * SLOT], ACT.Relu,
                                   bias=b1c[:, j:j + 1]).then_inc(t_ok, 1)

            def slot(s, last=False):
                w2_half(s, 0)
                relu(s, 0)
                w2_half(s, 1)
                relu(s, 1)
                relu(s, 2)
                relu(s, 3)
                if not last:
                    rows_hi(s + 1)
                    w1_half(s + 1, 0)
                    w1_half(s + 1, 1)

            act.wait_ge(scat, 16 * TILES)
            w1_half(0, 0)
            w1_half(0, 1)
            rows_hi(0)
            slot(0)
            with act.Fori(1, NSLOT - 1) as s:
                slot(s)
            slot(NSLOT - 1, True)
            with act.Fori(B_FIRST, GROUPS) as g:
                for i in range(MC):
                    step(g, i)

        @block.gpsimd
        def _(pool):
            pool.iota(w8[:], pattern=[[-1, E1]], base=E1, channel_multiplier=0,
                      allow_small_or_imprecise_dtypes=True).then_inc(r_io, 1)
            pool.iota(k256[:], pattern=[[SLOT, T // SLOT]], base=0, channel_multiplier=0,
                      allow_small_or_imprecise_dtypes=True).then_inc(r_io, 1)
            pool.iota(s_io[:], pattern=[[1, NSLOT + 1]], base=0, channel_multiplier=0,
                      allow_small_or_imprecise_dtypes=True).then_inc(r_io, 1)

            def xs(g, i):
                n = MC * g + i
                if not (zero(g) and i < 2):
                    pool.wait_ge(scan_ok, n - 1)
                pool.wait_ge(act_g, 3 * n + 2)
                pool.tensor_tensor(xs_b[:, i % 2, :], act_o[:, i % 2, 0, :], act_o[:, i % 2, 1, :], ALU.mult).then_inc(xs_ok, 1)

            def mix(g, i):
                c = i % DC
                if i >= 4:
                    pool.wait_ge(acc_ok, 6 * g + i - 3)
                if i >= MC - DC and not zero(g):
                    pool.wait_ge(fin_full, g)
                pool.wait_ge(hw_ok, MC * g + i + 1)
                dst = accT if i >= MC - DC else accO
                pool.tensor_tensor(dst[:, c, :], accO[:, c, :], hw_b[:, i % 2, :], ALU.add).then_inc(acc_ok, 1)

            def body(g):
                xs(g, 0)
                for i in range(MC):
                    if i + 1 < MC:
                        xs(g, i + 1)
                    if isinstance(g, int) and g == 1:
                        if i == 0:
                            pool.wait_ge(r_pos, 1)
                            pool.wait_ge(xn_in, 16)
                        for t in range(4 * i, 4 * i + 4):
                            pool.indirect_dma_start(out=xs_d, out_offset=bass.IndirectOffsetOnAxis(ap=pos_i[:, t:t + 1].bitcast(U32), axis=0),
                                                    in_=xn1_all[:, t, :], in_offset=None).then_inc(scat, 16)
                    if i >= DC:
                        mix(g, i)

            for g in range(B_FIRST):
                body(g)

            def w2_half(s, h):
                pool.wait_ge(w2_hi, 2 * s + h + 1)
                j = slice(h * HALF2, (h + 1) * HALF2)
                pool.tensor_tensor(w2_l[:, j, :], raw2[:, j, :], w2_h[:, j, :].bitcast(F32), ALU.subtract).then_inc(w2_lo, 1)

            pool.wait_ge(scat, 16 * TILES)
            with pool.Fori(0, NSLOT) as s:
                for h in (0, 1):
                    w2_half(s, h)

            def gather(g, dst, done):
                for j in range(JT):
                    pool.indirect_dma_start(out=dst[:, j, :], out_offset=None, in_=y_d,
                                            in_offset=bass.IndirectOffsetOnAxis(ap=(idx4[:, j:j + 1] if not zero(g) else pos_i[:, j:j + 1]).bitcast(U32), axis=0)).then_inc(done, 16)

            pool.wait_ge(y_st, 16 * NSLOT)
            gather(0, y0, y0_in)
            def gather_before(g):
                wait_alone(pool, fin_ok, g - 1)
                pool.tensor_copy(idx4[:], pos_i[:, bass.ds((g - 1) * JT, JT)]).then_inc(idx_ok, 1)
                wait_alone(pool, idx_ok, g - B_FIRST + 1)
                gather(None, y_b, y_in)

            with pool.Fori(B_FIRST, GROUPS) as g:
                gather_before(g)
                body(g)
            gather_before(GROUPS)

        @block.vector
        def _(dve):
            steps = [0]

            def link(ins):
                steps[0] += 1
                ins.then_inc(r_v, 1)
                dve.wait_ge(r_v, steps[0])

            def split_late(i):
                _, _, hi, lo = chunks[late[i]]
                dve.wait_ge(wb_hi, i + 1)
                dve.tensor_tensor(lo, staged(late[i]), hi.bitcast(F32), ALU.subtract).then_inc(wb_lo, 1)

            def mixture_weights():
                gl = logits[:, :, 0:M]
                link(dve.memset(rank[:], 0.0))
                for j in range(M):
                    for lo_m, hi_m, op in ((0, j, ALU.is_gt), (j + 1, M, ALU.is_ge)):
                        if lo_m < hi_m:
                            r = (P, TILES, hi_m - lo_m)
                            link(dve.tensor_tensor(cmp4[:, :, lo_m:hi_m], gl[:, :, j:j + 1].to_broadcast(r),
                                                   gl[:, :, lo_m:hi_m], op))
                            link(dve.tensor_tensor(rank[:, :, lo_m:hi_m], rank[:, :, lo_m:hi_m],
                                                   cmp4[:, :, lo_m:hi_m], ALU.add))
                link(dve.tensor_reduce(top[:, 0, :], gl, AX.X, ALU.max))
                link(dve.scalar_tensor_tensor(out=cmp4[:], in0=rank[:], scalar=1.0, in1=gl, op0=ALU.is_equal, op1=ALU.mult))
                link(dve.tensor_reduce(top[:, 1, :], cmp4[:], AX.X, ALU.add))
                dve.tensor_tensor(top[:, 3, :], top[:, 0, :], top[:, 1, :], ALU.subtract).then_inc(r_top, 1)

            def mixture_finish():
                dve.wait_ge(r_sig, 2)
                r = (P, TILES, M)
                link(dve.scalar_tensor_tensor(out=cmp4[:], in0=rank[:], scalar=0.0,
                                              in1=top[:, 2, :].unsqueeze(2).to_broadcast(r), op0=ALU.is_equal, op1=ALU.mult))
                link(dve.scalar_tensor_tensor(out=rank[:], in0=rank[:], scalar=1.0,
                                              in1=top[:, 1, :].unsqueeze(2).to_broadcast(r), op0=ALU.is_equal, op1=ALU.mult))
                dve.tensor_tensor(combm[:].rearrange("p m t -> p t m"), cmp4[:], rank[:], ALU.add).then_inc(r_comb, 1)

            def choose_expert():
                r = (P, TILES, E1)
                dve.wait_ge(r_io, 3)
                link(dve.tensor_tensor(el[:], logits[:, :, M:NL], ebias[:].unsqueeze(1).to_broadcast(r), ALU.add))
                link(dve.tensor_reduce(rmax[:], el[:], AX.X, ALU.max))
                link(dve.tensor_tensor(rt1[:], el[:], rmax[:].unsqueeze(2).to_broadcast(r), ALU.is_equal))
                link(dve.tensor_tensor(rt1[:], rt1[:], w8[:].unsqueeze(1).to_broadcast(r), ALU.mult))
                link(dve.tensor_reduce(rmax[:], rt1[:], AX.X, ALU.max))
                dve.tensor_tensor(onehot[:], rt1[:], rmax[:].unsqueeze(2).to_broadcast(r), ALU.is_equal).then_inc(r_hot, 1)

            def slot_rows():
                dve.wait_ge(r_cum, 1)
                cum = ps[:, 7, 0:256].rearrange("p (t e) -> p t e", e=E1)
                link(dve.tensor_copy(tot[:], ps[:, 7, 256:512].rearrange("p (t e) -> p e t", e=E1)))
                for e in range(E1):
                    link(dve.tensor_tensor_scan(incl[:, e, :], ones[:, 0:TILES], tot[:, e, :], 0.0, ALU.mult, ALU.add))
                r = (P, E1, T // SLOT)
                link(dve.tensor_tensor(cnt16[:], incl[:, :, TILES - 1:TILES].to_broadcast(r),
                                       k256[:].unsqueeze(1).to_broadcast(r), ALU.is_gt))
                link(dve.tensor_reduce(nsl[:], cnt16[:], AX.X, ALU.add))
                link(dve.tensor_tensor_scan(ends[:], ones[:, 0:E1], nsl[:], 0.0, ALU.mult, ALU.add))
                link(dve.tensor_tensor(nsl[:], ends[:], nsl[:], ALU.subtract))
                link(dve.tensor_tensor(incl[:], incl[:], tot[:], ALU.subtract))
                link(dve.tensor_scalar(out=nsl[:], in0=nsl[:], scalar1=float(SLOT), scalar2=None, op0=ALU.mult))
                link(dve.tensor_tensor(incl[:], incl[:], nsl[:].unsqueeze(2).to_broadcast((P, E1, TILES)), ALU.add))
                link(dve.tensor_tensor(rt1[:], cum, incl[:].rearrange("p e t -> p t e"), ALU.add))
                link(dve.tensor_tensor(rt1[:], rt1[:], onehot[:], ALU.mult))
                link(dve.tensor_reduce(rmax[:], rt1[:], AX.X, ALU.add))
                dve.tensor_copy(pos_i[:], rmax[:]).then_inc(r_pos, 1)
                se = (P, NSLOT + 1, E1)
                link(dve.tensor_tensor(cse[:], ends[:].unsqueeze(1).to_broadcast(se), s_io[:].unsqueeze(2).to_broadcast(se),
                                       ALU.is_le))
                link(dve.tensor_reduce(sef[:], cse[:], AX.X, ALU.add))
                dve.tensor_scalar(out=slot_e[:], in0=sef[:], scalar1=float(E1 - 1), scalar2=None,
                                  op0=ALU.min).then_inc(r_slot, 1)

            def step(g, i):
                n = MC * g + i
                m, c = divmod(i, DC)
                dve.wait_ge(act_g, 3 * n + 3)
                dve.tensor_scalar(out=a_b[:, i % 2, :], in0=act_o[:, i % 2, 2, :], scalar1=0.998, scalar2=0.001,
                                  op0=ALU.mult, op1=ALU.add).then_inc(a_ok, 1)
                dve.wait_ge(a_ok, n + 1)
                dve.wait_ge(xs_ok, n + 1)
                if not zero(g):
                    dve.wait_ge(hst, n - MC + 1)
                dve.tensor_tensor_scan(h_b[:, i % 2, :], a_b[:, i % 2, :], xs_b[:, i % 2, :], hstate[:, i:i + 1],
                                       ALU.mult, ALU.add).then_inc(scan_ok, 1)
                dve.wait_ge(scan_ok, n + 1)
                dve.tensor_copy(hstate[:, i:i + 1], h_b[:, i % 2, GT - 1:GT]).then_inc(hst, 1)
                if i == 0:
                    dve.wait_ge(comb_in, 16 * (g + 1))
                if i >= 4:
                    dve.wait_ge(acc_ok, 6 * g + i - 3)
                elif not zero(g):
                    dve.wait_ge(acc_ok, 6 * g)
                dst = accO[:, c, :] if m == 0 else hw_b[:, i % 2, :]
                dve.tensor_tensor(dst, h_b[:, i % 2, :], comb_b[:, bass.ds(ring(g), 1), m, :].rearrange("p a t -> p (a t)"),
                                  ALU.mult).then_inc(hw_ok, 1)

            def total(g):
                dve.wait_ge(x1b_in, 16 * (g + 1))
                dve.wait_ge(fin_full, g + 1)
                if zero(g):
                    dve.tensor_tensor(first_res[:], side4, x1_b[:], ALU.add).then_inc(fin_ok, 1)
                    return
                dve.wait_ge(out_st, 16 * (g - 1))
                dve.tensor_tensor(res[:], side4, x1_b[:], ALU.add).then_inc(fin_sum, 1)
                dve.wait_ge(fin_sum, g)
                dve.wait_ge(y_in, 64 * g)
                dve.tensor_tensor(res[:], res[:], y_b[:], ALU.add).then_inc(fin_ok, 1)

            mixture_weights()
            for i in range(2):
                split_late(i)
            mixture_finish()
            for g in range(B_FIRST):
                for i in range(MC):
                    if g == 0 and i < 4:
                        split_late(i + 2)
                    if g == 0 and i == 0:
                        choose_expert()
                    if g == 0 and i == 4:
                        slot_rows()
                    step(g, i)
                    if g and i == 3:
                        total(g - 1)

            def w1_half(s, h):
                dve.wait_ge(w1_hi, 2 * s + h + 1)
                f = slice(h * HALF1, (h + 1) * HALF1)
                dve.tensor_tensor(w1_l[:, :, f], raw1[:, :, f], w1_h[:, :, f].bitcast(F32), ALU.subtract).then_inc(w1_lo, 1)

            def rows_lo(s):
                dve.wait_ge(sT_hi, s + 1)
                dve.tensor_tensor(sT_l[:].rearrange("p c t -> p (c t)"), ps[:, 6, :],
                                  sT_h[:].rearrange("p c t -> p (c t)").bitcast(F32), ALU.subtract).then_inc(sT_ok, 1)

            def parts(s, q):
                n = FJ // 2 * s + q
                dve.wait_ge(t_ok, 2 * (n + 1))
                j = slice(2 * q, 2 * q + 2)
                dve.tensor_copy(eT_h[:, j, :], t32[:, j, :]).then_inc(e_hi, 1)
                dve.wait_ge(e_hi, n + 1)
                dve.tensor_tensor(eT_l[:, j, :], t32[:, j, :], eT_h[:, j, :].bitcast(F32), ALU.subtract).then_inc(e_ok, 1)

            def slot(s, last=False):
                for q in range(FJ // 2):
                    parts(s, q)
                if not last:
                    rows_lo(s + 1)
                    w1_half(s + 1, 0)
                    w1_half(s + 1, 1)
                dve.wait_ge(b2_in, 16 * (s + 1))
                if not zero(s):
                    dve.wait_ge(y_st, 16 * s)
                dve.wait_ge(l2_full, s + 1)
                dve.tensor_tensor(y_sb[:], ps[:, 4:6, 0:D], b2b[:].unsqueeze(1).to_broadcast((P, ST, D)),
                                  ALU.add).then_inc(ys_ok, 1)

            w1_half(0, 0)
            w1_half(0, 1)
            rows_lo(0)
            slot(0)
            with dve.Fori(1, NSLOT - 1) as s:
                slot(s)
            slot(NSLOT - 1, True)
            with dve.Fori(B_FIRST, GROUPS) as g:
                for i in range(MC):
                    step(g, i)
                    if i == 3:
                        total(g - 1)
            total(GROUPS - 1)
            dve.wait_ge(y0_in, 64)
            dve.tensor_tensor(first_res[:], first_res[:], y0[:], ALU.add).then_inc(fin_ok, 1)


def kernel(**inputs):
    import concourse.bacc as bacc
    from concourse.bass_utils import run_bass_kernel_spmd

    def c(x):
        return np.ascontiguousarray(x)

    i = inputs
    host = {
        "x": c(i["L0_attn_x"]),
        "wq": c(i["L0_attn_W_q"].T),
        "wk": c(i["L0_attn_W_k"].T),
        "wg": c(i["L0_attn_W_g"].T),
        "wv": c(np.concatenate([i["L0_attn_W_v"].T, i["L0_ffn_expert_sel"].T], axis=1)),
        "wo": c(i["L0_attn_W_o"].T),
        "log_decay": c(i["L0_attn_log_decay"]),
        "keys": c(np.transpose(i["L0_ffn_keys"], (1, 0, 2)).reshape(D, E0 * H0)),
        "values": c(i["L0_ffn_values"]),
        "wgvd": c(np.stack([i["L1_attn_Wg"], i["L1_attn_Wv"], i["L1_attn_Wd"]])),
        "scan_bias": c(np.stack([i["L1_attn_bg"], i["L1_attn_bv"], i["L1_attn_bd"]]).reshape(3, MC, P).transpose(2, 0, 1)),
        "gates": c(np.concatenate([i["L1_attn_gate_W"], i["L1_ffn_gate_w"].T], axis=1)),
        "gate_b": c(i["L1_ffn_gate_b"]),
        "expert_bias": c(i["L1_ffn_expert_bias"]),
        "w1": c(i["L1_ffn_w1"]),
        "b1": c(i["L1_ffn_b1"].reshape(E1, FJ, P).transpose(0, 2, 1)),
        "w2": c(i["L1_ffn_w2"]),
        "b2": c(i["L1_ffn_b2"]),
    }
    nc = bacc.Bacc("TRN2", target_bir_lowering=False, num_devices=1)
    aps = {n: nc.dram_tensor(n, v.shape, mybir.dt.from_np(v.dtype), kind="ExternalInput").ap() for n, v in host.items()}
    out = nc.dram_tensor("out", (1, T, D), F32, kind="ExternalOutput").ap()
    build(nc, aps, out)
    r = run_bass_kernel_spmd(nc, [host], core_ids=[0])
    return r.results[0]["out"]
```

```python
import numpy as np
import concourse.bass as bass
from concourse import mybir

F32 = mybir.dt.float32
F32R = mybir.dt.float32r
I32 = mybir.dt.int32
U32 = mybir.dt.uint32
ALU = mybir.AluOpType
ACT = mybir.ActivationFunctionType
AX = mybir.AxisListType

P = 128
T, D = 4096, 256
DC = D // P
GT = 512
GROUPS = T // GT
JT = GT // P
TILES = T // P
E0, H0 = 16, 128
M = 4
MC = M * DC
E1, F1 = 8, 1024
FJ = F1 // P
SLOT = 256
ST = SLOT // P
NSLOT = T // SLOT + E1 - 1
CHUNK = 32
NL = M + E1
VS = D + E0
EPS = 1e-5
XN_RING = 4
N_LATE = 4
N_STAGE = 4
B_FIRST = 3
KB = 1024


def build(nc, a, out):
    base = (nc.sbuf_base + 31) // 32 * 32

    class Region:

        def __init__(self, start):
            self.at = start

        def __call__(self, name, shape, dtype):
            t = nc.alloc_sbuf_tensor_at(name, shape, dtype, offset=self.at)
            self.at += (int(np.prod(shape[1:])) * 4 + 31) // 32 * 32
            return t

    def sem(name):
        return nc.alloc_semaphore(name)

    keep = Region(base)
    ident = keep("ident", [P, P], F32)
    tri = keep("tri", [P, P], F32)
    ones = keep("ones", [P, P], F32)
    maskT = keep("maskT", [P, P], F32)
    scan_bias = keep("scan_bias", [P, 3, MC], F32)
    gate_bias = keep("gate_bias", [P, JT, NL], F32)
    ebias = keep("ebias", [P, E1], F32)
    logits = keep("logits", [P, TILES, NL], F32)
    gw_h = keep("gw_h", [P, DC, NL], F32R)
    gw_l = keep("gw_l", [P, DC, NL], F32R)
    gw_raw = keep("gw_raw", [P, DC, NL], F32)
    hstate = keep("hstate", [P, MC], F32)
    neg_half = keep("neg_half", [P, JT], F32)
    pos_i = keep("pos_i", [P, TILES], I32)
    slot_e = keep("slot_e", [P, NSLOT + 1], I32)
    zeros = keep("zeros", [P, D], F32)
    decay = keep("decay", [P, 2], F32)
    WB_h = [[None] * 3 for _ in range(M)]
    WB_l = [[None] * 3 for _ in range(M)]
    for m in range(2):
        for w in range(3):
            WB_h[m][w] = keep(f"WB_h{m}{w}", [P, DC, D], F32R)
            WB_l[m][w] = keep(f"WB_l{m}{w}", [P, DC, D], F32R)
    start_a = keep.at

    def mix_buffers(region, tag, t0, t1):
        n = t1 - t0
        return dict(t0=t0, t1=t1,
                    rank=region("rank" + tag, [P, n, M], F32), cmp4=region("cmp4" + tag, [P, n, M], F32),
                    top=region("top" + tag, [P, 4, n], F32), comb=region("comb" + tag, [P, n, M], F32),
                    combT=region("combT" + tag, [P, P], F32))

    ra = Region(start_a)
    x_in = ra("x_in", [P, JT, D], F32)
    mix1 = mix_buffers(Region(start_a), "1", 0, TILES - JT)
    xn = ra("xn", [P, JT, D], F32)
    xT_h = ra("xT_h", [P, DC, GT], F32R)
    xT_l = ra("xT_l", [P, DC, GT], F32R)
    xT = ra("xT", [P, DC, GT], F32)
    qT = Region(ra.at)("qT", [P, DC, GT], F32)
    oT_h = ra("oT_h", [P, DC, GT], F32R)
    oT_l = ra("oT_l", [P, DC, GT], F32R)
    sig_g = ra("sig_g", [P, DC, GT], F32)
    v32 = ra("v32", [P, JT, D], F32)
    s32 = ra("s32", [P, JT, P], F32)
    sel = ra("sel", [P, JT, E0], F32)
    hT_h = ra("hT_h", [P, 2, GT], F32R)
    hT_l = ra("hT_l", [P, 2, GT], F32R)
    acc = ra("acc", [P, JT, D], F32)
    ytmp = ra("ytmp", [P, 2, 2, D], F32)
    otmp = sig_g[:, 0, :].rearrange("p (j d) -> p j d", j=2)
    stats0 = ra("stats0", [P, JT, 6], F32)
    mv0 = ra("mv0", [P, JT, 2], F32)
    rstd0 = ra("rstd0", [P, JT], F32)
    stage = ra("stage", [P, N_STAGE, 4 * D], F32)
    PW = {}
    for n in ("qk", "g", "v", "o"):
        cols = VS if n == "v" else D
        PW[n] = (ra(f"w{n}_h", [P, DC, cols], F32R), ra(f"w{n}_l", [P, DC, cols], F32R))
    keys_h = ra("keys_h", [P, DC, E0 * H0], F32R)
    keys_l = ra("keys_l", [P, DC, E0 * H0], F32R)
    vals_h = ra("vals_h", [P, E0, D], F32R)
    vals_l = ra("vals_l", [P, E0, D], F32R)
    at_post = ra.at
    x1 = ra("x1", [P, JT, D], F32)
    xn1 = ra("xn1", [P, JT, D], F32)
    nT_h = ra("nT_h", [P, DC, GT], F32R)
    nT_l = ra("nT_l", [P, DC, GT], F32R)
    stats1 = ra("stats1", [P, JT, 6], F32)
    mv1 = ra("mv1", [P, JT, 2], F32)
    rstd1 = ra("rstd1", [P, JT], F32)
    lgT = ra("lgT", [P, GT], F32)
    end_a = ra.at
    x1T = nc.alloc_sbuf_tensor_at("x1T", [P, 2, 2, DC, GT], F32R, offset=end_a - 8 * KB)

    rb = Region(start_a)
    stage_b = rb("stage_b", [P, N_LATE, DC, D], F32)
    for m in range(2, M):
        for w in range(3):
            WB_h[m][w] = rb(f"WB_h{m}{w}", [P, DC, D], F32R)
            WB_l[m][w] = rb(f"WB_l{m}{w}", [P, DC, D], F32R)
    comb_b = rb("comb_b", [P, 2, JT, M, P], F32)
    x1_b = rb("x1_b", [P, JT, D], F32)
    y_b = rb("y_b", [P, JT, D], F32)
    first_res = rb("first_res", [P, 2, JT, D], F32)
    accT = rb("accT", [P, DC, GT], F32)
    accO = rb("accO", [P, DC, GT], F32)
    idx4 = rb("idx4", [P, JT], I32)
    at_bc = rb.at
    act_o = rb("act_o", [P, 2, 3, GT], F32)
    a_b = rb("a_b", [P, 2, GT], F32)
    xs_b = rb("xs_b", [P, 2, GT], F32)
    h_b = rb("h_b", [P, 2, GT], F32)
    hw_b = rb("hw_b", [P, 2, GT], F32)
    rc = Region(at_bc)
    t32 = rc("t32", [P, FJ, SLOT], F32)
    eT_h = rc("eT_h", [P, FJ, SLOT], F32R)
    eT_l = rc("eT_l", [P, FJ, SLOT], F32R)
    rc.at = max(rc.at, rb.at)
    at_raw = rc.at
    raw1 = rc("raw1", [P, DC, F1], F32)
    raw2 = rc("raw2", [P, FJ, D], F32)
    rows = rc("rows", [P, ST, D], F32)
    sT_h = rc("sT_h", [P, DC, SLOT], F32R)
    sT_l = rc("sT_l", [P, DC, SLOT], F32R)
    y_sb = rc("y_sb", [P, ST, D], F32)
    b1c = rc("b1c", [P, FJ], F32)
    b2b = rc("b2b", [P, D], F32)
    w1_h = rc("w1_h", [P, DC, F1], F32R)
    w1_l = rc("w1_l", [P, DC, F1], F32R)
    at_w2 = rc.at
    w2_h = rc("w2_h", [P, FJ, D], F32R)
    w2_l = rc("w2_l", [P, FJ, D], F32R)
    first_y = Region(at_raw)("first_y", [P, 2, JT, D], F32)
    xn1_r = Region(at_w2)("xn1_r", [P, XN_RING, JT, D], F32)
    rr = Region(at_raw)
    mix2 = mix_buffers(rr, "2", TILES - JT, TILES)
    el = rr("el", [P, TILES, E1], F32)
    onehot = rr("onehot", [P, TILES, E1], F32)
    rt1 = rr("rt1", [P, TILES, E1], F32)
    w8 = rr("w8", [P, E1], F32)
    tot = rr("tot", [P, E1, TILES], F32)
    incl = rr("incl", [P, E1, TILES], F32)
    rmax = rr("rmax", [P, TILES], F32)
    k256 = rr("k256", [P, T // SLOT], F32)
    cnt16 = rr("cnt16", [P, E1, T // SLOT], F32)
    nsl = rr("nsl", [P, E1], F32)
    ends = rr("ends", [P, E1], F32)
    s_io = rr("s_io", [P, NSLOT + 1], F32)
    cse = rr("cse", [P, NSLOT + 1, E1], F32)
    sef = rr("sef", [P, NSLOT + 1], F32)
    assert rr.at - at_raw <= 16 * KB and end_a + 8 * KB <= nc.sbuf_usable_end
    assert rc.at <= end_a - 8 * KB and max(rb.at, at_raw + 16 * KB) <= at_post

    ps = nc.alloc_psum_tensor("ps", [P, 8, 512], F32)
    side2 = ps[:, 6:8, :]
    side4 = ps[:, 6:8, :].rearrange("p b (j d) -> p (b j) d", j=2)

    def yb(k, j):
        return ps[:, 2 + 2 * (k % 2) + j // 2, (j % 2) * D:(j % 2 + 1) * D]

    x1_d = nc.dram_tensor("x1_d", (GROUPS, P, JT, D), F32, kind="Internal").ap()
    xn1_d = nc.dram_tensor("xn1_d", (GROUPS, P, JT, D), F32, kind="Internal").ap()
    xT1_d = nc.dram_tensor("xT1_d", (GROUPS, 2, P, DC, GT), F32, kind="Internal").ap()
    comb_d = nc.dram_tensor("comb_d", (TILES, M, P), F32, kind="Internal").ap()
    xs_d = nc.dram_tensor("xs_d", (NSLOT * SLOT, D), F32, kind="Internal").ap()
    y_d = nc.dram_tensor("y_d", (NSLOT * SLOT, D), F32, kind="Internal").ap()

    x_v = a["x"][0].rearrange("(g j p) d -> g p j d", p=P, j=JT)
    out_v = out[0].rearrange("(g j p) d -> g p j d", p=P, j=JT)
    xs_v = xs_d.rearrange("(s i p) d -> s p i d", p=P, i=ST)
    y_v = y_d.rearrange("(s i p) d -> s p i d", p=P, i=ST)

    def cpo(w):
        return w.rearrange("(c p) o -> p c o", p=P)

    chunks = {}
    order = []

    def add_chunk(name, src, hi, lo):
        chunks[name] = (len(order), src, hi, lo)
        order.append(name)

    keys_v = cpo(a["keys"])
    vals_v = a["values"].rearrange("e h v -> h e v")
    for n in ("keys0", "v", "qk", "vals0", "g", "keys1", "vals1", "keys2", "vals2", "o", "keys3", "vals3"):
        if n.startswith("keys"):
            s = slice(int(n[4]) * 4 * H0, int(n[4]) * 4 * H0 + 4 * H0)
            add_chunk(n, keys_v[:, :, s], keys_h[:, :, s], keys_l[:, :, s])
        elif n.startswith("vals"):
            s = slice(int(n[4]) * 4, int(n[4]) * 4 + 4)
            add_chunk(n, vals_v[:, s, :], vals_h[:, s, :], vals_l[:, s, :])
        elif n == "qk":
            add_chunk(n, a["wqk"].rearrange("w (c p) i -> p (w c) i", p=P), PW[n][0][:], PW[n][1][:])
        else:
            add_chunk(n, cpo(a["w" + n]), PW[n][0][:], PW[n][1][:])
    n_a = len(order)
    for m in range(M):
        for w in range(3):
            add_chunk(f"b{m}{w}", cpo(a["wgvd"][w, m]), WB_h[m][w][:], WB_l[m][w][:])

    n_b = n_a + 6

    def staged(name):
        n, src, _, _ = chunks[name]
        d1, d2 = src.shape[1], src.shape[2]
        if n >= n_b:
            return stage_b[:, (n - n_b) % N_LATE]
        return stage[:, n % N_STAGE, 0:d1 * d2].rearrange("p (a b) -> p a b", a=d1)

    wqk_raw = stage[:, order.index("qk") % N_STAGE].rearrange("p (w c i) -> p w c i", w=2, c=DC)
    wqk_ps = ps[:, 2, :].rearrange("p (c i) -> p c i", c=DC)

    ticks = sem("ticks")
    w_in = [sem(f"w_in{b}") for b in range(N_STAGE)]
    w_hi, w_lo = sem("w_hi"), sem("w_lo")
    qk_full = sem("qk_full")
    small_in = sem("small_in")
    gw_ready = sem("gw_ready")
    consts = sem("consts")
    dec_in, dec_s, mask_v, mask_p = sem("dec_in"), sem("dec_s"), sem("mask_v"), sem("mask_p")
    z_out = sem("z_out")
    x_ld = sem("x_ld")
    bn0, mvs0, pe0, rs0, xn0 = sem("bn0"), sem("mvs0"), sem("pe0"), sem("rs0"), sem("xn0")
    bn1, mvs1, pe1, rs1, xn1s = sem("bn1"), sem("mvs1"), sem("pe1"), sem("rs1"), sem("xn1s")
    side_full, side_hi, side_free = sem("side_full"), sem("side_hi"), sem("side_free")
    xT_sum = sem("xT_sum")
    sel_ok = sem("sel_ok")
    o_gate, o_hi, o_23 = sem("o_gate"), sem("o_hi"), sem("o_23")
    h_full, h_hi, h_lo = sem("h_full"), sem("h_hi"), sem("h_lo")
    y_f01, y_f23 = sem("y_f01"), sem("y_f23")
    acc_iv, acc_ip = sem("acc_iv"), sem("acc_ip")
    acc01, y_23, acc23 = sem("acc01"), sem("y_23"), sem("acc23")
    x1_st, xn1_st, xT1_st = sem("x1_st"), sem("xn1_st"), sem("xT1_st")
    x1T_in = sem("x1T_in")
    wb_hi, wb_lo2, wb_lo3 = sem("wb_hi"), sem("wb_lo2"), sem("wb_lo3")
    b_full, act_g = sem("b_full"), sem("act_g")
    r_m, r_top, r_sig, r_comb, comb_st = (sem(n) for n in ("r_m", "r_top", "r_sig", "r_comb", "comb_st"))

    N01 = 2 * E0 + 1
    N23 = E0 + 1
    O_STEP = 11

    USES = ["v01", "v23", "q", "g", "s", "t1", "lg", "o", "lt", "op", "t0", "t0b"]
    POST = ("t1", "lg", "lt")
    HI_USES = ["t1", "t0", "t0b"]

    def use(g, name, first=False):
        names = [u for u in USES if not (first and u in POST)]
        start = 2 if first else 12 * g - 1
        return start + names.index(name)

    def hi_use(g, name, first=False):
        names = [u for u in HI_USES if not (first and u == "t1")]
        start = 2 if first else 3 * g + 1
        return start + names.index(name)

    def freed(g, name, first=False):
        names = [u for u in USES if u != "op" and not (first and u in POST)]
        start = 2 if first else 11 * g - 1
        return start + names.index(name) + 1

    def post_use(g, name):
        if isinstance(g, int) and g == GROUPS - 1:
            n = 2 + POST.index(name)
            return use(g, "op") + n, hi_use(g, "t0"), freed(g, "lt") + n
        return use(g + 1, name), hi_use(g + 1, "t1"), freed(g + 1, name)

    def wait_alone(eng, s, value):
        eng.wait_ge(s, value)
        eng.sem_inc(ticks, 1)

    def mm3(pe, dst, wh, wl, xh, xl, start, stop):
        pe.matmul(dst, wh, xh, start=start, stop=False)
        pe.matmul(dst, wh, xl, start=False, stop=False)
        return pe.matmul(dst, wl, xh, start=False, stop=stop)

    def rstd(pool, mv, veps, rs, mvs, pes, rss, g):
        wait_alone(pool, mvs, JT * (g + 1))
        pool.tensor_scalar(out=veps, in0=mv[:, :, 1], scalar1=EPS, scalar2=1.0, op0=ALU.add,
                           op1=ALU.mult).then_inc(pes, 1)
        pool.wait_ge(pes, g + 1)
        pool.tensor_tensor(rs[:], veps, neg_half[:], ALU.pow).then_inc(rss, 1)

    def t_hi(act, n, dst, src):
        act.wait_ge(side_full, n + 1)
        act.activation(dst, src, ACT.Copy).then_inc(side_hi, 1)

    def logits_T(act, n):
        act.wait_ge(side_full, n + 1)
        act.activation(lgT[0:NL, :], ps[0:NL, 6, :], ACT.Copy).then_inc(side_free, 1)

    def ln_stats(dve, x, st, bn, tiles=range(JT)):
        for j in tiles:
            dve.bn_stats(st[:, j, :], x[:, j, :]).then_inc(bn, 1)

    def ln_aggr(dve, st, mv, bn, mvs, g):
        wait_alone(dve, bn, JT * (g + 1))
        for j in range(JT):
            dve.bn_aggr(mv[:, j, :], st[:, j, :]).then_inc(mvs, 1)

    def ln_norm(dve, dst, x, mv, rs, rss, done, g, tiles=range(JT)):
        dve.wait_ge(rss, g + 1)
        for j in tiles:
            dve.tensor_scalar(out=dst[:, j, :], in0=x[:, j, :], scalar1=mv[:, j, 0:1],
                              scalar2=rs[:, j:j + 1], op0=ALU.subtract, op1=ALU.mult).then_inc(done, 1)

    def lo_of(dve, nh, dst, hi, src):
        dve.wait_ge(side_hi, nh + 1)
        dve.tensor_tensor(dst, src, hi.bitcast(F32), ALU.subtract).then_inc(side_free, 1)

    def ln1_stats(dve, g, tiles):
        if 0 in tiles:
            dve.wait_ge(acc01, N01 * (g + 1))
        else:
            dve.wait_ge(acc23, N23 * (g + 1))
        ln_stats(dve, x1, stats1, bn1, tiles)

    def ln1_norm(dve, g, tiles):
        dve.wait_ge(xn1_st, 1 + 16 * g)
        ln_norm(dve, xn1, x1, mv1, rstd1, rs1, xn1s, g, tiles)

    def gate_logits(dve, g):
        dve.wait_ge(side_full, post_use(g, "lt")[0] + 1)
        dve.tensor_tensor(logits[:, bass.ds(g * JT, JT), :], ps[:, 6, 0:JT * NL].rearrange("p (j n) -> p j n", j=JT),
                          gate_bias[:], ALU.add).then_inc(side_free, 1)

    def transposes(pe, src, c):
        for j in range(JT):
            last = pe.transpose(side2[:, c, j * P:(j + 1) * P], src[:, j, c * P:(c + 1) * P], ident[:])
        return last

    def post_transposes(pe, g):
        pe.wait_ge(xn1s, JT * (g + 1))
        if isinstance(g, int) and g == GROUPS - 1:
            pe.wait_ge(side_free, freed(g, "lt") + 1)
        else:
            pe.wait_ge(side_free, freed(g + 1, "s"))
        for c in range(DC):
            last = transposes(pe, xn1, c)
        last.then_inc(side_full, 1)

    def post_logits(pe, g):
        pe.wait_ge(side_free, post_use(g, "t1")[2])
        for c in range(DC):
            last_mm = mm3(pe, ps[0:NL, 6, :], gw_h[:, c, :], gw_l[:, c, :], nT_h[:, c, :], nT_l[:, c, :],
                          c == 0, c == DC - 1)
        last_mm.then_inc(side_full, 1)

    def post_rows(pe, g):
        if isinstance(g, int) and g == GROUPS - 1:
            wait_alone(pe, side_free, post_use(g, "lg")[2])
        else:
            wait_alone(pe, side_free, freed(g + 1, "o"))
        for j in range(JT):
            last_mm = pe.transpose(ps[:, 6, j * NL:(j + 1) * NL], lgT[0:NL, j * P:(j + 1) * P], ident[0:NL, 0:NL])
        last_mm.then_inc(side_full, 1)

    def mixture_weights(dve, link, mx):
        n, rank, cmp4, top = mx["t1"] - mx["t0"], mx["rank"], mx["cmp4"], mx["top"]
        gl = logits[:, mx["t0"]:mx["t1"], 0:M]
        link(dve.memset(rank[:], 0.0))
        for j in range(M):
            for lo_m, hi_m, op in ((0, j, ALU.is_gt), (j + 1, M, ALU.is_ge)):
                if lo_m < hi_m:
                    r = (P, n, hi_m - lo_m)
                    link(dve.tensor_tensor(cmp4[:, :, lo_m:hi_m], gl[:, :, j:j + 1].to_broadcast(r),
                                           gl[:, :, lo_m:hi_m], op))
                    link(dve.tensor_tensor(rank[:, :, lo_m:hi_m], rank[:, :, lo_m:hi_m],
                                           cmp4[:, :, lo_m:hi_m], ALU.add))
        link(dve.tensor_reduce(top[:, 0, :], gl, AX.X, ALU.max))
        link(dve.scalar_tensor_tensor(out=cmp4[:], in0=rank[:], scalar=1.0, in1=gl, op0=ALU.is_equal, op1=ALU.mult))
        link(dve.tensor_reduce(top[:, 1, :], cmp4[:], AX.X, ALU.add))
        dve.tensor_tensor(top[:, 3, :], top[:, 0, :], top[:, 1, :], ALU.subtract).then_inc(r_top, 1)

    def mixture_finish(dve, link, mx, part):
        n, rank, cmp4, top = mx["t1"] - mx["t0"], mx["rank"], mx["cmp4"], mx["top"]
        dve.wait_ge(r_sig, 2 * part)
        r = (P, n, M)
        link(dve.scalar_tensor_tensor(out=cmp4[:], in0=rank[:], scalar=0.0,
                                      in1=top[:, 2, :].unsqueeze(2).to_broadcast(r), op0=ALU.is_equal, op1=ALU.mult))
        link(dve.scalar_tensor_tensor(out=rank[:], in0=rank[:], scalar=1.0,
                                      in1=top[:, 1, :].unsqueeze(2).to_broadcast(r), op0=ALU.is_equal, op1=ALU.mult))
        dve.tensor_tensor(mx["comb"][:], cmp4[:], rank[:], ALU.add).then_inc(r_comb, 1)

    def mixture_sigmoids(act, mx, part):
        act.wait_ge(r_top, part)
        act.activation(mx["top"][:, 2, :], mx["top"][:, 3, :], ACT.Sigmoid).then_inc(r_sig, 1)
        act.activation(mx["top"][:, 1, :], mx["top"][:, 3, :], ACT.Sigmoid, scale=-1.0).then_inc(r_sig, 1)

    def mixture_rows(mx):
        return (mx["t1"] - mx["t0"]) * M

    def mixture_transpose(pe, mx, part):
        pe.wait_ge(r_comb, part)
        return pe.transpose(ps[0:mixture_rows(mx), 6, 0:P], mx["comb"][:].rearrange("p t m -> p (t m)"), ident[:])

    def mixture_copy(act, mx):
        r = mixture_rows(mx)
        return act.activation(mx["combT"][0:r, :], ps[0:r, 6, 0:P], ACT.Copy)

    def mixture_store(sp, mx):
        sp.dma_start(comb_d[mx["t0"]:mx["t1"]].rearrange("t m p -> (t m) p"),
                     mx["combT"][0:mixture_rows(mx), :]).then_inc(comb_st, 16)

    late = order[n_b:]

    def lo_late(eng, i):
        _, _, hi, lo = chunks[late[i]]
        eng.wait_ge(wb_hi, i + 1)
        return eng.tensor_tensor(lo, staged(late[i]), hi.bitcast(F32), ALU.subtract)

    def zero(g):
        return isinstance(g, int) and g == 0

    def ring(g):
        return (g + 1) % 2

    def scan_products(pe, g, i):
        m, c = divmod(i, DC)
        if not (zero(g) and i < 2):
            pe.wait_ge(act_g, 3 * (MC * g + i - 1))
        for w in range(3):
            if zero(g) and m >= 2:
                pe.wait_ge(wb_lo2 if m == 2 else wb_lo3, w + 1)
            s = slice(c * P, (c + 1) * P)
            for k in range(DC):
                last_mm = mm3(pe, ps[:, 3 * (i % 2) + w, :], WB_h[m][w][:, k, s], WB_l[m][w][:, k, s],
                              x1T[:, bass.ds(ring(g), 1), 0, k, :], x1T[:, bass.ds(ring(g), 1), 1, k, :],
                              k == 0, k == DC - 1)
            last_mm.then_inc(b_full, 1)

    def x1_store(sp, g):
        wait_alone(sp, acc01, N01 * (g + 1))
        wait_alone(sp, acc23, N23 * (g + 1))
        sp.dma_start(x1_d[g], x1[:]).then_inc(x1_st, 16)

    def xn1_store(sp, g):
        wait_alone(sp, xn1s, JT * (g + 1))
        sp.dma_start(xn1_d[g], xn1[:]).then_inc(xn1_st, 16)

    def xT1_store(sp, g):
        wait_alone(sp, side_free, post_use(g, "t1")[2])
        sp.dma_start(xT1_d[g, 0], nT_h[:].bitcast(F32)).then_inc(xT1_st, 16)
        sp.dma_start(xT1_d[g, 1], nT_l[:].bitcast(F32)).then_inc(xT1_st, 16)

    with nc.Block("A") as block:
        FIRST_SPLITS = {0: ["g"], 1: ["keys1"], 2: ["vals1"], 3: ["keys2"], 4: ["vals2"], 5: ["o"],
                        6: ["keys3"], 10: ["vals3"]}
        FIRST_LOADS = ["qk", "keys0", "v", "vals0"]
        LAST_SPLITS = {2: ["b00"], 4: ["b01"], 6: ["b02"], 8: ["b10"], 10: ["b11"], 12: ["b12"]}

        @block.sync
        def _(sp):
            sp.dma_start(x_in[:], x_v[0]).then_inc(x_ld, 16)
            sp.sem_inc(xn1_st, 1)
            sp.sem_inc(xT1_st, 1)

            def weight(name):
                n, src, _, _ = chunks[name]
                if n >= N_STAGE:
                    sp.wait_ge(w_lo, n - N_STAGE + 1)
                sp.dma_start(staged(name), src).then_inc(w_in[n % N_STAGE], 16)

            def body(g, first, last):
                if not last:
                    wait_alone(sp, acc_iv, g + 1)
                    wait_alone(sp, acc_ip, g + 1)
                    sp.dma_start(x_in[:], x_v[g + 1]).then_inc(x_ld, 16)
                if not first:
                    x1_store(sp, g - 1)
                    xn1_store(sp, g - 1)
                    xT1_store(sp, g - 1)

            for name in FIRST_LOADS + order[len(FIRST_LOADS):n_a]:
                if name == "o":
                    body(0, True, False)
                weight(name)
            with sp.Fori(1, GROUPS - 1) as g:
                body(g, False, False)
            for name in order[n_a:n_b]:
                weight(name)
            body(GROUPS - 1, False, True)
            sp.wait_ge(xT1_st, 1 + 32)
            for part in (0, 1):
                sp.dma_start(x1T[:, 1, part, :, :].bitcast(F32), xT1_d[0, part]).then_inc(x1T_in, 16)
            sp.wait_ge(side_free, freed(GROUPS - 1, "lt") + 1)
            mixture_store(sp, mix1)
            sp.wait_ge(x1_st, 16 * (GROUPS - 1))
            sp.wait_ge(xn1_st, 1 + 16 * (GROUPS - 1))
            sp.wait_ge(xT1_st, 1 + 32 * (GROUPS - 1))
            sp.wait_ge(z_out, 16)
            sp.wait_ge(comb_st, 16)

        @block.gpsimd
        def _(pool):
            pool.memset(ident[:], 0.0).then_inc(consts, 1)
            pool.memset(ones[:], 1.0).then_inc(consts, 1)
            pool.memset(tri[:], 1.0).then_inc(consts, 1)
            pool.memset(zeros[:], 0.0).then_inc(consts, 1)
            pool.memset(neg_half[:], -0.5).then_inc(consts, 1)
            pool.memset(hstate[:], 0.0).then_inc(consts, 1)
            pool.memset(gate_bias[:], 0.0).then_inc(consts, 1)
            pool.wait_ge(consts, 7)
            pool.affine_select(out=ident[:], in_=ident[:], compare_op=ALU.not_equal, fill=1.0, base=0,
                               pattern=[[-1, P]], channel_multiplier=1).then_inc(consts, 1)
            pool.affine_select(out=tri[:], in_=tri[:], compare_op=ALU.is_gt, fill=0.0, base=0,
                               pattern=[[1, P]], channel_multiplier=-1).then_inc(consts, 1)

            def trim_mask():
                pool.wait_ge(mask_v, 1)
                blocks = maskT[:].rearrange("p (b c) -> p b c", c=CHUNK)
                pool.affine_select(out=blocks, in_=blocks, compare_op=ALU.is_ge, fill=0.0, base=0,
                                   pattern=[[-CHUNK, P // CHUNK], [0, CHUNK]], channel_multiplier=1).then_inc(mask_p, 1)
                pool.wait_ge(mask_p, 1)
                pool.affine_select(out=blocks, in_=blocks, compare_op=ALU.is_ge, fill=0.0, base=CHUNK - 1,
                                   pattern=[[CHUNK, P // CHUNK], [0, CHUNK]], channel_multiplier=-1).then_inc(mask_p, 1)

            def body(g, first, last):
                if not first:
                    pool.wait_ge(acc23, N23 * g)
                pool.wait_ge(xn0, JT * (g + 1))
                pool.tensor_tensor(acc[:, 2:4, :], x_in[:, 2:4, :], xn[:, 2:4, :], ALU.add).then_inc(acc_ip, 1)
                pool.wait_ge(acc_ip, g + 1)
                n = 0
                for k in range(E0):
                    pool.wait_ge(y_23, 2 * (E0 * g + k + 1))
                    pool.wait_ge(acc23, N23 * g + n)
                    if k == E0 - 1 and not first:
                        pool.wait_ge(x1_st, 16 * g)
                    dst = x1 if k == E0 - 1 else acc
                    pool.tensor_tensor(dst[:, 2:4, :], acc[:, 2:4, :], ytmp[:, k % 2, :, :], ALU.add).then_inc(acc23, 1)
                    n += 1
                    if k == 0:
                        pool.wait_ge(side_free, 2 if first else freed(g, "v01") - 1)
                        if not first:
                            pool.wait_ge(side_full, use(g, "v01"))
                        pool.tensor_tensor(xT[:], xT_h[:].bitcast(F32), xT_l[:].bitcast(F32), ALU.add).then_inc(xT_sum, 1)
                    if k == 1 and first:
                        trim_mask()
                    if k == 1 and not first:
                        rstd(pool, mv1, stats1[:, :, 0], rstd1, mvs1, pe1, rs1, g - 1)
                    if k == 7 and not last:
                        rstd(pool, mv0, stats0[:, :, 0], rstd0, mvs0, pe0, rs0, g + 1)
                    if k == O_STEP:
                        pool.wait_ge(o_23, g + 1)
                        pool.wait_ge(acc23, N23 * g + n)
                        pool.tensor_tensor(acc[:, 2:4, :], acc[:, 2:4, :], otmp[:], ALU.add).then_inc(acc23, 1)
                        n += 1

            rstd(pool, mv0, stats0[:, :, 0], rstd0, mvs0, pe0, rs0, 0)
            body(0, True, False)
            with pool.Fori(1, GROUPS - 1) as g:
                body(g, False, False)
            body(GROUPS - 1, False, True)

        @block.scalar
        def _(act):
            def on_all(row):
                return row.rearrange("(o n) -> o n", o=1).to_broadcast((P, row.shape[0]))

            act.dma_start(decay[:, 1:2], on_all(a["log_decay"][0:1])).then_inc(dec_in, 16)
            act.dma_start(gw_raw[:], cpo(a["gates"])).then_inc(small_in, 16)
            act.dma_start(scan_bias[:], a["scan_bias"]).then_inc(small_in, 16)
            act.dma_start(ebias[:], on_all(a["expert_bias"])).then_inc(small_in, 16)
            act.wait_ge(consts, 7)
            for j in range(JT):
                act.dma_start(gate_bias[:, j, M:NL], on_all(a["gate_b"])).then_inc(small_in, 16)

            def split(name):
                n, _, hi, _ = chunks[name]
                act.wait_ge(w_in[n % N_STAGE], 16 * (n // N_STAGE + 1))
                if name == "qk":
                    act.wait_ge(qk_full, 1)
                act.activation(hi, wqk_ps if name == "qk" else staged(name), ACT.Copy).then_inc(w_hi, 1)

            def relu_hi(g, k, first):
                act.wait_ge(h_full, E0 * g + k + 1)
                if not (first and k < 2):
                    act.wait_ge(y_f23, E0 * g + k - 1)
                act.activation(hT_h[:, k % 2, :], ps[:, k % 2, :], ACT.Relu).then_inc(h_hi, 1)

            def xT_hi(g, c, first):
                t_hi(act, use(g, "t0", first) + c, xT_h[:, c, :], ps[:, 6 + c, :])

            def values(g, half, first):
                n = use(g, "v01" if half == 0 else "v23", first)
                act.wait_ge(side_full, n + 1)
                act.activation(sel[:, 2 * half:2 * half + 2, :], side2[:, :, D:VS], ACT.Sigmoid).then_inc(sel_ok, 1)
                act.activation(v32[:, 2 * half:2 * half + 2, :], side2[:, :, 0:D], ACT.Copy).then_inc(side_free, 1)

            def body(g, first, last):
                splits = FIRST_SPLITS if first else LAST_SPLITS if last else {}
                relu_hi(g, 0, first)
                if not first:
                    act.wait_ge(acc01, N01 * g)
                values(g, 0, first)
                if first:
                    split("vals0")
                relu_hi(g, 1, first)
                values(g, 1, first)
                for k in range(E0):
                    if 1 <= k < E0 - 1:
                        relu_hi(g, k + 1, first)
                    if k == E0 - 2 and not last:
                        act.wait_ge(xT_sum, g + 1)
                        xT_hi(g, 0, first)
                    if k == E0 - 1 and not last:
                        xT_hi(g, 1, first)
                    act.wait_ge(y_f23, E0 * g + k + 1)
                    if not (first and k < 2):
                        act.wait_ge(acc23, N23 * g + k - 1 + (1 if k - 2 >= O_STEP else 0))
                    if k == 0:
                        act.wait_ge(sel_ok, 2 * (g + 1))
                    for j in (2, 3):
                        act.activation(ytmp[:, k % 2, j - 2, :], yb(k, j), ACT.Copy,
                                       scale=sel[:, j, k:k + 1]).then_inc(y_23, 1)
                    if k == 2:
                        act.wait_ge(side_full, use(g, "g", first) + 1)
                        act.activation(sig_g[:], side2, ACT.Sigmoid).then_inc(side_free, 1)
                    if k == 5 and not first:
                        act.wait_ge(xT1_st, 1 + 32 * (g - 1))
                        t_hi(act, use(g, "t1"), nT_h[:], side2)
                    if k == 6 and not first:
                        logits_T(act, post_use(g - 1, "lg")[0])
                    if k == 7:
                        act.wait_ge(o_gate, g + 1)
                        act.activation(oT_h[:], sig_g[:], ACT.Copy).then_inc(o_hi, 1)
                    if k == O_STEP:
                        act.wait_ge(side_full, use(g, "op", first) + 1)
                        if not first:
                            act.wait_ge(acc23, N23 * (g - 1) + O_STEP + 2)
                        act.activation(otmp[:], side4[:, 2:4, :], ACT.Copy).then_inc(o_23, 1)
                    if k == 11 and last:
                        mixture_sigmoids(act, mix1, 1)
                    if k == E0 - 2 and last:
                        act.wait_ge(side_full, use(g, "op") + 2)
                        mixture_copy(act, mix1).then_inc(side_free, 1)
                    for name in splits.get(k, []):
                        split(name)

            act.wait_ge(dec_in, 16)
            act.activation(decay[:, 0:1], decay[:, 1:2], ACT.Sigmoid).then_inc(dec_s, 1)
            split("keys0")
            for c in range(DC):
                t_hi(act, c, xT_h[:, c, :], ps[:, 6 + c, :])
            split("v")
            split("qk")
            act.wait_ge(small_in, 16 * (3 + JT))
            act.activation(gw_h[:], gw_raw[:], ACT.Copy).then_inc(gw_ready, 1)
            body(0, True, False)
            act.dma_start(xs_d.rearrange("(r p) d -> p r d", p=P),
                          zeros[:].unsqueeze(1).to_broadcast((P, NSLOT * ST, D))).then_inc(z_out, 16)
            with act.Fori(1, GROUPS - 1) as g:
                body(g, False, False)
            body(GROUPS - 1, False, True)

        @block.vector
        def _(dve):
            linked = [0]

            def link(ins):
                linked[0] += 1
                ins.then_inc(r_m, 1)
                dve.wait_ge(r_m, linked[0])

            def split(name):
                n, _, hi, lo = chunks[name]
                dve.wait_ge(w_hi, n + 1)
                dve.tensor_tensor(lo, wqk_ps if name == "qk" else staged(name), hi.bitcast(F32),
                                  ALU.subtract).then_inc(w_lo, 1)

            def xT_lo(nh, c):
                lo_of(dve, nh + c, xT_l[:, c, :], xT_h[:, c, :], ps[:, 6 + c, :])

            def relu_lo(g, k):
                dve.wait_ge(h_hi, E0 * g + k + 1)
                dve.scalar_tensor_tensor(out=hT_l[:, k % 2, :], in0=ps[:, k % 2, :], scalar=0.0,
                                         in1=hT_h[:, k % 2, :].bitcast(F32), op0=ALU.max,
                                         op1=ALU.subtract).then_inc(h_lo, 1)

            def decay_mask():
                dve.wait_ge(dec_s, 1)
                dve.wait_ge(consts, 9)
                dve.tensor_tensor_scan(maskT[:], decay[:, 0:1].to_broadcast((P, P)), ident[:], 0.0, ALU.mult,
                                       ALU.add).then_inc(mask_v, 1)

            def body(g, first, last):
                splits = FIRST_SPLITS if first else LAST_SPLITS if last else {}
                relu_lo(g, 0)
                if first:
                    split("vals0")
                relu_lo(g, 1)
                dve.wait_ge(xn0, JT * (g + 1))
                dve.tensor_tensor(acc[:, 0:2, :], x_in[:, 0:2, :], xn[:, 0:2, :], ALU.add).then_inc(acc_iv, 1)
                dve.wait_ge(sel_ok, 2 * g + 2)
                dve.wait_ge(acc_iv, g + 1)
                n = 0
                for k in range(E0):
                    if 1 <= k < E0 - 1:
                        relu_lo(g, k + 1)
                    if k == E0 - 2 and not last:
                        xT_lo(hi_use(g, "t0", first), 0)
                    if k == E0 - 1 and not last:
                        xT_lo(hi_use(g, "t0", first), 1)
                    dve.wait_ge(y_f01, E0 * g + k + 1)
                    if k == E0 - 1 and not first:
                        dve.wait_ge(x1_st, 16 * g)
                    dst = x1 if k == E0 - 1 else acc
                    if k > 0:
                        dve.wait_ge(acc01, N01 * g + n)
                    for j in (0, 1):
                        dve.scalar_tensor_tensor(out=dst[:, j, :], in0=yb(k, j), scalar=sel[:, j, k:k + 1],
                                                 in1=acc[:, j, :], op0=ALU.mult, op1=ALU.add).then_inc(acc01, 1)
                        n += 1
                    if k == 1:
                        dve.wait_ge(side_full, use(g, "q", first) + 1)
                        dve.tensor_copy(qT[:], side2).then_inc(side_free, 1)
                    if k == 0 and not first:
                        ln1_stats(dve, g - 1, range(0, 2))
                    if k == 1 and not first:
                        ln1_stats(dve, g - 1, range(2, 4))
                        ln_aggr(dve, stats1, mv1, bn1, mvs1, g - 1)
                    if k == 3 and not first:
                        ln1_norm(dve, g - 1, range(0, 2))
                    if k == 4 and not first:
                        ln1_norm(dve, g - 1, range(2, 4))
                    if k == 4:
                        dve.wait_ge(side_full, use(g, "s", first) + 1)
                        if first:
                            dve.wait_ge(mask_p, 2)
                        dve.tensor_tensor(s32[:], ps[:, 6, :].rearrange("p (j c) -> p j c", j=JT),
                                          maskT[:].unsqueeze(1).to_broadcast((P, JT, P)), ALU.mult).then_inc(side_free, 1)
                    if k == 5 and not first:
                        lo_of(dve, hi_use(g, "t1"), nT_l[:], nT_h[:], side2)
                    if k == 10 and not first:
                        gate_logits(dve, g - 1)
                    if k == 7:
                        dve.wait_ge(side_full, use(g, "o", first) + 1)
                        dve.tensor_tensor(sig_g[:], side2, sig_g[:], ALU.mult).then_inc(o_gate, 1)
                    if k == 8:
                        dve.wait_ge(o_hi, g + 1)
                        dve.tensor_tensor(oT_l[:], sig_g[:], oT_h[:].bitcast(F32), ALU.subtract).then_inc(side_free, 1)
                    if k == 5 and not last:
                        dve.wait_ge(x_ld, 16 * (g + 2))
                        ln_stats(dve, x_in, stats0, bn0, range(0, 2))
                    if k == 6 and not last:
                        ln_stats(dve, x_in, stats0, bn0, range(2, 4))
                    if k == 7 and not last:
                        ln_aggr(dve, stats0, mv0, bn0, mvs0, g + 1)
                    if k in (9, 10) and not last:
                        if k == 9:
                            dve.wait_ge(acc_ip, g + 1)
                        ln_norm(dve, xn, x_in, mv0, rstd0, rs0, xn0, g + 1, range(2 * (k - 9), 2 * (k - 8)))
                    if k == O_STEP:
                        dve.wait_ge(side_full, use(g, "op", first) + 1)
                        dve.wait_ge(acc01, N01 * g + n)
                        dve.tensor_tensor(acc[:, 0:2, :], side4[:, 0:2, :], acc[:, 0:2, :], ALU.add).then_inc(acc01, 1)
                        n += 1
                    for name in splits.get(k, []):
                        split(name)
                    if k == 0 and first:
                        decay_mask()
                    if k == 5 and first:
                        dve.wait_ge(gw_ready, 1)
                        dve.tensor_tensor(gw_l[:], gw_raw[:], gw_h[:].bitcast(F32), ALU.subtract).then_inc(gw_ready, 1)
                    if k == 10 and last:
                        dve.wait_ge(side_free, freed(g, "lt"))
                        mixture_weights(dve, link, mix1)
                    if k == 12 and last:
                        mixture_finish(dve, link, mix1, 1)

            dve.wait_ge(x_ld, 16)
            ln_stats(dve, x_in, stats0, bn0)
            ln_aggr(dve, stats0, mv0, bn0, mvs0, 0)
            ln_norm(dve, xn, x_in, mv0, rstd0, rs0, xn0, 0)
            split("keys0")
            for c in range(DC):
                xT_lo(0, c)
            split("v")
            split("qk")
            body(0, True, False)
            with dve.Fori(1, GROUPS - 1) as g:
                body(g, False, False)
            body(GROUPS - 1, False, True)

        @block.tensor
        def _(pe):
            def body(g, first, last):
                def ready(name):
                    pe.wait_ge(side_free, freed(g, name, first))

                def weights(name):
                    if first:
                        pe.wait_ge(w_lo, chunks[name][0] + 1)

                def up(k):
                    weights(f"keys{k // 4}")
                    if not (first and k < 2):
                        pe.wait_ge(h_lo, E0 * g + k - 1)
                    s = slice(k * H0, (k + 1) * H0)
                    for c in range(DC):
                        if k == 0:
                            pe.wait_ge(side_free, xT_ready - 1 + c)
                        last = mm3(pe, ps[:, k % 2, :], keys_h[:, c, s], keys_l[:, c, s], xT_h[:, c, :], xT_l[:, c, :],
                                   c == 0, c == DC - 1)
                    last.then_inc(h_full, 1)

                def down(k):
                    weights(f"vals{k // 4}")
                    pe.wait_ge(h_lo, E0 * g + k + 1)
                    for half, done in ((0, y_f01), (1, y_f23)):
                        if not (first and k < 2):
                            if half == 0:
                                pe.wait_ge(acc01, N01 * g + 2 * (k - 1) + (1 if k - 2 >= O_STEP + 1 else 0))
                            else:
                                pe.wait_ge(y_23, 2 * (E0 * g + k - 1))
                        for j in (2 * half, 2 * half + 1):
                            s = slice(j * P, (j + 1) * P)
                            pe.matmul(yb(k, j), hT_h[:, k % 2, s], vals_h[:, k, :], start=True, stop=False)
                            pe.matmul(yb(k, j), hT_h[:, k % 2, s], vals_l[:, k, :], start=False, stop=False)
                            last_mm = pe.matmul(yb(k, j), hT_l[:, k % 2, s], vals_h[:, k, :], start=False, stop=True)
                        last_mm.then_inc(done, 1)

                def project(n):
                    weights(n)
                    for o in range(DC):
                        for c in range(DC):
                            s = slice(o * P, (o + 1) * P)
                            last_mm = mm3(pe, side2[:, o, :], PW[n][0][:, c, s], PW[n][1][:, c, s], xT_h[:, c, :],
                                          xT_l[:, c, :], c == 0, c == DC - 1)
                    last_mm.then_inc(side_full, 1)

                def rows_times(dst, th, tl, j, wh, wl):
                    s = slice(j * P, (j + 1) * P)
                    for c in range(DC):
                        pe.matmul(dst, th[:, c, s], wh[:, c, :], start=c == 0, stop=False)
                        pe.matmul(dst, th[:, c, s], wl[:, c, :], start=False, stop=False)
                        last_mm = pe.matmul(dst, tl[:, c, s], wh[:, c, :], start=False, stop=c == DC - 1)
                    return last_mm

                def values(half):
                    weights("v")
                    for j in (0, 1):
                        last_mm = rows_times(side2[:, j, 0:VS], xT_h, xT_l, 2 * half + j, *PW["v"])
                    last_mm.then_inc(side_full, 1)

                xT_ready = 2 if first else freed(g, "v01") - 1
                up(0)
                values(0)
                up(1)
                ready("v01")
                values(1)
                for k in range(E0):
                    if 1 <= k < E0 - 1:
                        up(k + 1)
                    down(k)
                    if k == 1:
                        ready("v23")
                        project("qk")
                    if k == 2:
                        ready("q")
                        project("g")
                    if k == 4:
                        ready("g")
                        pe.wait_ge(xT_sum, g + 1)
                        for j in range(JT):
                            s = slice(j * P, (j + 1) * P)
                            for c in range(DC):
                                last_mm = pe.matmul(ps[:, 6, s], xT[:, c, s], qT[:, c, s], start=c == 0,
                                                    stop=c == DC - 1)
                        last_mm.then_inc(side_full, 1)
                    if k == 5 and not first:
                        post_transposes(pe, g - 1)
                    if k == 6 and not first:
                        post_logits(pe, g - 1)
                    if k == 10 and not first:
                        post_rows(pe, g - 1)
                    if k == 7:
                        ready("s" if first else "lg")
                        for c in range(DC):
                            for j in range(JT):
                                last_mm = pe.matmul(side2[:, c, j * P:(j + 1) * P], v32[:, j, c * P:(c + 1) * P],
                                                    s32[:, j, :], start=True, stop=True)
                        last_mm.then_inc(side_full, 1)
                    if k == O_STEP:
                        ready("o" if first else "lt")
                        weights("o")
                        for j in range(JT):
                            last_mm = rows_times(side4[:, j, :], oT_h, oT_l, j, *PW["o"])
                        last_mm.then_inc(side_full, 1)
                    if k == E0 - 3:
                        if not last:
                            pe.wait_ge(xn0, JT * (g + 2))
                        pe.wait_ge(o_23, g + 1)
                        pe.wait_ge(acc01, N01 * g + 2 * (O_STEP + 1) + 1)
                        if last:
                            mixture_transpose(pe, mix1, 1).then_inc(side_full, 1)
                        else:
                            transposes(pe, xn, 0).then_inc(side_full, 1)
                    if k == E0 - 2 and not last:
                        transposes(pe, xn, 1).then_inc(side_full, 1)

            pe.wait_ge(w_in[chunks["qk"][0] % N_STAGE], 16)
            for j in range(DC):
                for o in range(DC):
                    last_mm = pe.matmul(wqk_ps[:, j, :], wqk_raw[:, 0, o, j * P:(j + 1) * P], wqk_raw[:, 1, o, :],
                                        start=o == 0, stop=o == DC - 1)
            last_mm.then_inc(qk_full, 1)
            pe.wait_ge(consts, 8)
            pe.wait_ge(xn0, JT)
            for c in range(DC):
                transposes(pe, xn, c).then_inc(side_full, 1)
            body(0, True, False)
            pe.wait_ge(gw_ready, 2)
            with pe.Fori(1, GROUPS - 1) as g:
                body(g, False, False)
            body(GROUPS - 1, False, True)
            pe.wait_ge(x1T_in, 32)
            pe.wait_ge(w_lo, n_b)
            pe.wait_ge(h_lo, E0 * GROUPS)
            pe.wait_ge(acc01, N01 * GROUPS - 2)
            scan_products(pe, 0, 0)

    wb_in = [sem(f"wb_in{b}") for b in range(N_LATE)]
    comb_in, x1b_in = sem("comb_in"), sem("x1b_in")
    xs_ok, a_ok, scan_ok, hst, hw_ok, acc_ok = (sem(n) for n in ("xs_ok", "a_ok", "scan_ok", "hst", "hw_ok", "acc_ok"))
    fin_full, fin_sum, fin_ok, out_st = (sem(n) for n in ("fin_full", "fin_sum", "fin_ok", "out_st"))
    first_ok, first_st = sem("first_ok"), sem("first_st")
    idx_ok, y_in, first_y_in = sem("idx_ok"), sem("y_in"), sem("first_y_in")
    r_io, r_v, r_ct, r_cs = sem("r_io"), sem("r_v"), sem("r_ct"), sem("r_cs")
    r_hot, r_cum, r_pos, r_slot = (sem(n) for n in ("r_hot", "r_cum", "r_pos", "r_slot"))
    xn_in = [sem(f"xn_in{b}") for b in range(XN_RING)]
    scat = [sem(f"scat{b}") for b in range(XN_RING)]
    r1_in, r2_in, b1_in, b2_in, rows_in = (sem(n) for n in ("r1_in", "r2_in", "b1_in", "b2_in", "rows_in"))
    w1_hi, w1_lo, w2_hi, w2_lo = (sem(n) for n in ("w1_hi", "w1_lo", "w2_hi", "w2_lo"))
    T_full, sT_hi, sT_ok = sem("T_full"), sem("sT_hi"), sem("sT_ok")
    l1_full, t_ok, e_hi, e_ok, l2_full, ys_ok, y_st = (
        sem(n) for n in ("l1_full", "t_ok", "e_hi", "e_ok", "l2_full", "ys_ok", "y_st"))

    w1_v = a["w1"].rearrange("e (c p) f -> e p c f", p=P)
    w2_v = a["w2"].rearrange("e (j p) d -> e p j d", p=P)
    HALF1, HALF2 = F1 // 2, FJ // 2
    HI_LATE = {0: [0, 1], 1: [2], 2: [3], 3: [4], 4: [5]}
    LO_LATE_M2 = {0: [0], 1: [1], 2: [2]}
    LO_LATE_M3 = {2: [3], 3: [4], 4: [5]}

    def rows_step(g):
        return {1: 4, 2: 3}.get(g, 2) if isinstance(g, int) else 2

    def all_scattered(eng):
        for b in range(XN_RING):
            eng.wait_ge(scat[b], 16 * TILES // XN_RING)

    with nc.Block("RBC") as block:

        @block.sync
        def _(sp):
            def load_x1T(g):
                if not zero(g):
                    wait_alone(sp, x1T_in, 32 * g)
                if not (isinstance(g, int) and g < 2):
                    wait_alone(sp, b_full, 3 * MC * (g - 1))
                for part in (0, 1):
                    sp.dma_start(x1T[:, bass.ds(ring(g), 1), part, :, :].bitcast(F32),
                                 xT1_d[bass.ds(g, 1), part].rearrange("a p c t -> p a c t")).then_inc(x1T_in, 16)

            def load_comb(g):
                if not zero(g):
                    wait_alone(sp, comb_in, 16 * g)
                if not (isinstance(g, int) and g < 2):
                    wait_alone(sp, hw_ok, MC * (g - 1))
                sp.dma_start(comb_b[:, bass.ds(ring(g), 1)],
                             comb_d[bass.ds(g * JT, JT)].rearrange("(o t) m p -> o t m p", o=1).unsqueeze(0)
                             .to_broadcast((P, 1, JT, M, P))).then_inc(comb_in, 16)

            def body(g, last=False):
                if not last:
                    load_x1T(g + 1)
                    load_comb(g + 1)
                if not zero(g):
                    wait_alone(sp, fin_ok, g)
                    if not (isinstance(g, int) and g <= B_FIRST - 1):
                        sp.dma_start(out_v[bass.ds(g - 1, 1)].rearrange("a p j d -> p (a j) d"),
                                     x1_b[:]).then_inc(out_st, 16)
                        wait_alone(sp, out_st, 16 * (g - 2))
                sp.dma_start(x1_b[:], x1_d[bass.ds(g, 1)].rearrange("a p j d -> p (a j) d")).then_inc(x1b_in, 16)

            def load_late(i):
                if i >= N_LATE:
                    sp.wait_ge(wb_lo2, i - N_LATE + 1)
                sp.dma_start(staged(late[i]), chunks[late[i]][1]).then_inc(wb_in[i % N_LATE], 16)

            def load_xn1(g):
                if g >= XN_RING:
                    sp.wait_ge(scat[g % XN_RING], 16 * JT * (g // XN_RING))
                sp.dma_start(xn1_r[:, g % XN_RING], xn1_d[g]).then_inc(xn_in[g % XN_RING], 16)

            g = GROUPS - 1
            load_late(0)
            load_late(1)
            load_comb(0)
            load_late(2)
            load_late(3)
            x1_store(sp, g)
            xn1_store(sp, g)
            load_late(4)
            load_late(5)
            xT1_store(sp, g)
            sp.wait_ge(x1_st, 16 * GROUPS)
            sp.wait_ge(xn1_st, 1 + 16 * GROUPS)
            sp.wait_ge(xT1_st, 1 + 32 * GROUPS)
            sp.wait_ge(side_free, post_use(g, "lt")[2])
            body(0)
            for g in range(XN_RING):
                load_xn1(g)
            sp.wait_ge(r_cs, 1)
            mixture_store(sp, mix2)
            body(1)
            sp.wait_ge(comb_st, 32)
            for g in range(XN_RING, GROUPS):
                load_xn1(g)

            def slot(s):
                load_rows(s)
                e = raw1_of(s)
                if not (isinstance(s, int) and s < 2):
                    finish(s - 2)
                b2_of(s - 1)
                raw2_b1(s, e)

            def raw1_of(s):
                if not zero(s):
                    wait_alone(sp, w1_lo, 2 * s)
                e = sp.value_load(slot_e[0:1, bass.ds(s, 1)], min_val=0, max_val=E1 - 1)
                sp.dma_start(raw1[:], w1_v[bass.ds(e, 1)].rearrange("a p c f -> p (a c) f")).then_inc(r1_in, 16)
                return e

            def load_rows(s):
                if not zero(s):
                    wait_alone(sp, T_full, s)
                sp.dma_start(rows[:], xs_v[bass.ds(s, 1)].rearrange("a p i d -> p (a i) d")).then_inc(rows_in, 16)

            def raw2_b1(s, e):
                if not zero(s):
                    wait_alone(sp, w2_lo, 2 * s)
                sp.dma_start(raw2[:], w2_v[bass.ds(e, 1)].rearrange("a p j d -> p (a j) d")).then_inc(r2_in, 16)
                if not zero(s):
                    wait_alone(sp, t_ok, FJ * s)
                sp.dma_start(b1c[:], a["b1"][bass.ds(e, 1)].rearrange("a p j -> p (a j)")).then_inc(b1_in, 16)

            def finish(s):
                wait_alone(sp, ys_ok, s + 1)
                sp.dma_start(y_v[bass.ds(s, 1)].rearrange("a p i d -> p (a i) d"), y_sb[:]).then_inc(y_st, 16)

            def b2_of(s):
                e = sp.value_load(slot_e[0:1, bass.ds(s, 1)], min_val=0, max_val=E1 - 1)
                sp.dma_start(b2b[:], a["b2"][bass.ds(e, 1)].to_broadcast((P, D))).then_inc(b2_in, 16)

            sp.wait_ge(r_slot, 1)
            raw2_b1(0, raw1_of(0))
            all_scattered(sp)
            load_rows(0)
            body(2)
            slot(1)
            with sp.Fori(2, NSLOT) as s:
                slot(s)
            finish(NSLOT - 2)
            b2_of(NSLOT - 1)
            finish(NSLOT - 1)
            with sp.Fori(B_FIRST, GROUPS - 1) as g:
                body(g)
            body(GROUPS - 1, True)
            for g in (0, 1):
                sp.wait_ge(first_ok, g + 1)
                sp.dma_start(out_v[g], first_res[:, g]).then_inc(first_st, 16)
            for half in (0, 1):
                sp.wait_ge(fin_ok, GROUPS + half)
                tiles = slice(2 * half, 2 * half + 2)
                sp.dma_start(out_v[GROUPS - 1][:, tiles, :], x1_b[:, tiles, :]).then_inc(out_st, 16)
            sp.wait_ge(first_st, 32)
            sp.wait_ge(out_st, 16 * (GROUPS - 1))

        @block.tensor
        def _(pe):
            def to_rows(g):
                if zero(g):
                    pe.wait_ge(r_cs, 1)
                    pe.wait_ge(r_pos, 1)
                else:
                    pe.wait_ge(fin_ok, g)
                for c in range(DC):
                    pe.wait_ge(acc_ok, 6 * (g + 1) - DC + 1 + c)
                    for j in range(JT):
                        last_mm = pe.transpose(side4[:, j, c * P:(c + 1) * P], accT[:, c, j * P:(j + 1) * P], ident[:])
                last_mm.then_inc(fin_full, 1)

            def body(g):
                pe.wait_ge(x1T_in, 32 * (g + 1))
                for i in range(1 if zero(g) else 0, MC):
                    if i == 1 and not isinstance(g, int):
                        pe.wait_ge(ys_ok, NSLOT)
                    scan_products(pe, g, i)
                    if zero(g) and i == 2:
                        post_transposes(pe, GROUPS - 1)
                    if zero(g) and i == 4:
                        post_logits(pe, GROUPS - 1)
                    if zero(g) and i == 5:
                        post_rows(pe, GROUPS - 1)
                    if isinstance(g, int) and (g, i) == (1, 0):
                        pe.wait_ge(side_free, post_use(GROUPS - 1, "lt")[2])
                        mixture_transpose(pe, mix2, 2).then_inc(r_ct, 1)
                        pe.wait_ge(r_hot, 1)
                        hot = onehot[:].rearrange("p t e -> p (t e)")
                        pe.matmul(ps[:, 7, 0:256], tri[:], hot, start=True, stop=True)
                        pe.matmul(ps[:, 7, 256:512], ones[:], hot, start=True, stop=True).then_inc(r_cum, 1)
                    if i == rows_step(g) and not zero(g):
                        to_rows(g - 1)
                    if i == MC - 2 and isinstance(g, int) and g == B_FIRST - 1:
                        pe.wait_ge(fin_ok, g)
                        rows_T(0)

            def rows_T(s):
                pe.wait_ge(rows_in, 16 * (s + 1))
                if not zero(s):
                    pe.wait_ge(sT_ok, s)
                for c in range(DC):
                    for i in range(ST):
                        last_mm = pe.transpose(ps[:, 6, c * SLOT + i * P:c * SLOT + (i + 1) * P],
                                               rows[:, i, c * P:(c + 1) * P], ident[:])
                last_mm.then_inc(T_full, 1)

            def slot(s, last=False):
                pe.wait_ge(sT_ok, s + 1)
                for q in range(FJ // 2):
                    if not zero(s):
                        pe.wait_ge(t_ok, FJ * (s - 1) + 2 * q + 2)
                    elif q == 3:
                        pe.wait_ge(act_g, 3 * MC * B_FIRST)
                    if q in (0, 2):
                        pe.wait_ge(w1_lo, 2 * s + 1 + q // 2)
                    for j in (2 * q, 2 * q + 1):
                        f = slice(j * P, (j + 1) * P)
                        for c in range(DC):
                            last_mm = mm3(pe, ps[:, q, (j % 2) * SLOT:(j % 2 + 1) * SLOT], w1_h[:, c, f], w1_l[:, c, f],
                                          sT_h[:, c, :], sT_l[:, c, :], c == 0, c == DC - 1)
                    last_mm.then_inc(l1_full, 1)
                if not last:
                    rows_T(s + 1)
                if not zero(s):
                    pe.wait_ge(ys_ok, s)
                for j in range(FJ):
                    if j % 2 == 0:
                        pe.wait_ge(e_ok, FJ // 2 * s + j // 2 + 1)
                    if j in (0, HALF2):
                        pe.wait_ge(w2_lo, 2 * s + 1 + j // HALF2)
                    for i in range(ST):
                        r = slice(i * P, (i + 1) * P)
                        dst = ps[:, 4 + i, 0:D]
                        pe.matmul(dst, eT_h[:, j, r], w2_h[:, j, :], start=j == 0, stop=False)
                        pe.matmul(dst, eT_h[:, j, r], w2_l[:, j, :], start=False, stop=False)
                        last_mm = pe.matmul(dst, eT_l[:, j, r], w2_h[:, j, :], start=False, stop=j == FJ - 1)
                last_mm.then_inc(l2_full, 1)

            for g in range(B_FIRST):
                body(g)
            pe.wait_ge(act_g, 3 * MC * B_FIRST - 3)
            slot(0)
            with pe.Fori(1, NSLOT - 1) as s:
                slot(s)
            slot(NSLOT - 1, True)
            with pe.Fori(B_FIRST, GROUPS) as g:
                body(g)
            to_rows(GROUPS - 1)

        @block.scalar
        def _(act):
            def step(g, i):
                n = MC * g + i
                if not (zero(g) and i < 2):
                    act.wait_ge(xs_ok, n - 1)
                    act.wait_ge(a_ok, n - 1)
                for w, func in enumerate((ACT.Sigmoid, ACT.Tanh, ACT.Sigmoid)):
                    act.wait_ge(b_full, 3 * n + w + 1)
                    act.activation(act_o[:, i % 2, w, :], ps[:, 3 * (i % 2) + w, :], func,
                                   bias=scan_bias[:, w, i:i + 1]).then_inc(act_g, 1)
                if not (zero(g) and i < 2):
                    act.wait_ge(scan_ok, n - 1)
                act.wait_ge(act_g, 3 * n + 3)
                act.activation(a_b[:, i % 2, :], act_o[:, i % 2, 2, :], ACT.Copy, scale=0.998,
                               bias=0.001).then_inc(a_ok, 1)

            def split_late(i):
                name = late[i]
                act.wait_ge(wb_in[i % N_LATE], 16 * (i // N_LATE + 1))
                act.activation(chunks[name][2], staged(name), ACT.Copy).then_inc(wb_hi, 1)

            def w1_half(s, h):
                if h == 0:
                    act.wait_ge(r1_in, 16 * (s + 1))
                if not zero(s):
                    act.wait_ge(l1_full, FJ // 2 * (s - 1) + 2 * (h + 1))
                f = slice(h * HALF1, (h + 1) * HALF1)
                act.activation(w1_h[:, :, f], raw1[:, :, f], ACT.Copy).then_inc(w1_hi, 1)

            def w2_half(s, h):
                if h == 0:
                    act.wait_ge(r2_in, 16 * (s + 1))
                    if not zero(s):
                        act.wait_ge(l2_full, s)
                j = slice(h * HALF2, (h + 1) * HALF2)
                act.activation(w2_h[:, j, :], raw2[:, j, :], ACT.Copy).then_inc(w2_hi, 1)

            def rows_hi(s):
                act.wait_ge(T_full, s + 1)
                act.activation(sT_h[:].rearrange("p c t -> p (c t)"), ps[:, 6, :], ACT.Copy).then_inc(sT_hi, 1)

            def relu(s, q):
                act.wait_ge(l1_full, FJ // 2 * s + q + 1)
                if q == 0:
                    act.wait_ge(b1_in, 16 * (s + 1))
                if not zero(s):
                    act.wait_ge(e_ok, FJ // 2 * (s - 1) + q + 1)
                elif q == 0:
                    act.wait_ge(acc_ok, 6 * B_FIRST)
                for j in (2 * q, 2 * q + 1):
                    act.activation(t32[:, j, :], ps[:, q, (j % 2) * SLOT:(j % 2 + 1) * SLOT], ACT.Relu,
                                   bias=b1c[:, j:j + 1]).then_inc(t_ok, 1)

            def slot(s, last=False):
                w2_half(s, 0)
                relu(s, 0)
                w2_half(s, 1)
                relu(s, 1)
                relu(s, 2)
                relu(s, 3)
                if not last:
                    rows_hi(s + 1)
                    w1_half(s + 1, 0)
                    w1_half(s + 1, 1)

            g = GROUPS - 1
            for i in range(MC):
                step(0, i)
                for n in HI_LATE.get(i, []):
                    split_late(n)
                if i == 2:
                    act.wait_ge(xT1_st, 1 + 32 * g)
                    t_hi(act, post_use(g, "t1")[0], nT_h[:], side2)
                if i == 4:
                    logits_T(act, post_use(g, "lg")[0])
                if i == 6:
                    mixture_sigmoids(act, mix2, 2)
            for g in range(1, B_FIRST):
                for i in range(MC):
                    step(g, i)
                    if (g, i) == (1, 0):
                        act.wait_ge(r_ct, 1)
                        mixture_copy(act, mix2).then_inc(r_cs, 1)
                    if g == B_FIRST - 1 and i in (5, 6):
                        w1_half(0, i - 5)
                    if g == B_FIRST - 1 and i == MC - 2:
                        rows_hi(0)
            all_scattered(act)
            slot(0)
            with act.Fori(1, NSLOT - 1) as s:
                slot(s)
            slot(NSLOT - 1, True)
            with act.Fori(B_FIRST, GROUPS) as g:
                for i in range(MC):
                    step(g, i)

        @block.gpsimd
        def _(pool):
            pool.iota(w8[:], pattern=[[-1, E1]], base=E1, channel_multiplier=0,
                      allow_small_or_imprecise_dtypes=True).then_inc(r_io, 1)
            pool.iota(k256[:], pattern=[[SLOT, T // SLOT]], base=0, channel_multiplier=0,
                      allow_small_or_imprecise_dtypes=True).then_inc(r_io, 1)
            pool.iota(s_io[:], pattern=[[1, NSLOT + 1]], base=0, channel_multiplier=0,
                      allow_small_or_imprecise_dtypes=True).then_inc(r_io, 1)

            def xs(i):
                if i >= 2:
                    pool.wait_ge(scan_ok, i - 1)
                pool.wait_ge(act_g, 3 * i + 2)
                pool.tensor_tensor(xs_b[:, i % 2, :], act_o[:, i % 2, 0, :], act_o[:, i % 2, 1, :],
                                   ALU.mult).then_inc(xs_ok, 1)

            def mix(g, i):
                c = i % DC
                if i >= 4:
                    pool.wait_ge(acc_ok, 6 * g + i - 3)
                if i >= MC - DC and not zero(g):
                    pool.wait_ge(fin_full, g)
                pool.wait_ge(hw_ok, MC * g + i + 1)
                dst = accT if i >= MC - DC else accO
                pool.tensor_tensor(dst[:, c, :], accO[:, c, :], hw_b[:, i % 2, :], ALU.add).then_inc(acc_ok, 1)

            GATHER_STEP = 5
            SCATTER_AT = [(1, 1), (1, 2), (1, 3), (1, 4), (1, 6), (1, 7), (2, 0), (2, 2)]

            def scatter(g):
                if g == 0:
                    pool.wait_ge(r_pos, 1)
                pool.wait_ge(xn_in[g % XN_RING], 16 * (g // XN_RING + 1))
                for j in range(JT):
                    rows_of = bass.IndirectOffsetOnAxis(ap=pos_i[:, g * JT + j:g * JT + j + 1].bitcast(U32), axis=0)
                    pool.indirect_dma_start(out=xs_d, out_offset=rows_of, in_=xn1_r[:, g % XN_RING, j, :],
                                            in_offset=None).then_inc(scat[g % XN_RING], 16)

            def gather(dst, index, done):
                for j in range(JT):
                    rows_of = bass.IndirectOffsetOnAxis(ap=index[:, j:j + 1].bitcast(U32), axis=0)
                    pool.indirect_dma_start(out=dst[:, j, :], out_offset=None, in_=y_d,
                                            in_offset=rows_of).then_inc(done, 16)

            def gather_rows(g):
                wait_alone(pool, fin_ok, g)
                pool.tensor_copy(idx4[:], pos_i[:, bass.ds(g * JT, JT)]).then_inc(idx_ok, 1)
                wait_alone(pool, idx_ok, g - B_FIRST + 1)
                gather(y_b, idx4, y_in)

            def body(g):
                if zero(g):
                    xs(0)
                for i in range(MC):
                    if zero(g) and i + 1 < MC:
                        xs(i + 1)
                        for n in LO_LATE_M2.get(i, []):
                            lo_late(pool, n).then_inc(wb_lo2, 1)
                    if isinstance(g, int) and (g, i) in SCATTER_AT:
                        scatter(SCATTER_AT.index((g, i)))
                    if i == GATHER_STEP and not isinstance(g, int):
                        gather_rows(g)
                    if i >= DC:
                        mix(g, i)

            rstd(pool, mv1, stats1[:, :, 0], rstd1, mvs1, pe1, rs1, GROUPS - 1)
            for g in range(B_FIRST):
                body(g)

            def w2_half(s, h):
                pool.wait_ge(w2_hi, 2 * s + h + 1)
                j = slice(h * HALF2, (h + 1) * HALF2)
                pool.tensor_tensor(w2_l[:, j, :], raw2[:, j, :], w2_h[:, j, :].bitcast(F32), ALU.subtract).then_inc(w2_lo, 1)

            with pool.Fori(0, NSLOT) as s:
                for h in (0, 1):
                    w2_half(s, h)

            pool.wait_ge(y_st, 16 * NSLOT)
            gather(y_b, pos_i[:, (B_FIRST - 1) * JT:B_FIRST * JT], y_in)
            for g in (0, 1):
                gather(first_y[:, g], pos_i[:, g * JT:(g + 1) * JT], first_y_in)
            with pool.Fori(B_FIRST, GROUPS) as g:
                body(g)

        @block.vector
        def _(dve):
            steps = [0]

            def link(ins):
                steps[0] += 1
                ins.then_inc(r_v, 1)
                dve.wait_ge(r_v, steps[0])

            def split_late(i):
                lo_late(dve, i).then_inc(wb_lo3, 1)

            def choose_expert():
                r = (P, TILES, E1)
                dve.wait_ge(r_io, 3)
                dve.wait_ge(side_free, post_use(GROUPS - 1, "lt")[2])
                link(dve.tensor_tensor(el[:], logits[:, :, M:NL], ebias[:].unsqueeze(1).to_broadcast(r), ALU.add))
                link(dve.tensor_reduce(rmax[:], el[:], AX.X, ALU.max))
                link(dve.tensor_tensor(rt1[:], el[:], rmax[:].unsqueeze(2).to_broadcast(r), ALU.is_equal))
                link(dve.tensor_tensor(rt1[:], rt1[:], w8[:].unsqueeze(1).to_broadcast(r), ALU.mult))
                link(dve.tensor_reduce(rmax[:], rt1[:], AX.X, ALU.max))
                dve.tensor_tensor(onehot[:], rt1[:], rmax[:].unsqueeze(2).to_broadcast(r), ALU.is_equal).then_inc(r_hot, 1)

            def slot_rows():
                dve.wait_ge(r_cum, 1)
                cum = ps[:, 7, 0:256].rearrange("p (t e) -> p t e", e=E1)
                link(dve.tensor_copy(tot[:], ps[:, 7, 256:512].rearrange("p (t e) -> p e t", e=E1)))
                for e in range(E1):
                    link(dve.tensor_tensor_scan(incl[:, e, :], ones[:, 0:TILES], tot[:, e, :], 0.0, ALU.mult, ALU.add))
                r = (P, E1, T // SLOT)
                link(dve.tensor_tensor(cnt16[:], incl[:, :, TILES - 1:TILES].to_broadcast(r),
                                       k256[:].unsqueeze(1).to_broadcast(r), ALU.is_gt))
                link(dve.tensor_reduce(nsl[:], cnt16[:], AX.X, ALU.add))
                link(dve.tensor_tensor_scan(ends[:], ones[:, 0:E1], nsl[:], 0.0, ALU.mult, ALU.add))
                link(dve.tensor_tensor(nsl[:], ends[:], nsl[:], ALU.subtract))
                link(dve.tensor_tensor(incl[:], incl[:], tot[:], ALU.subtract))
                link(dve.tensor_scalar(out=nsl[:], in0=nsl[:], scalar1=float(SLOT), scalar2=None, op0=ALU.mult))
                link(dve.tensor_tensor(incl[:], incl[:], nsl[:].unsqueeze(2).to_broadcast((P, E1, TILES)), ALU.add))
                link(dve.tensor_tensor(rt1[:], cum, incl[:].rearrange("p e t -> p t e"), ALU.add))
                link(dve.tensor_tensor(rt1[:], rt1[:], onehot[:], ALU.mult))
                link(dve.tensor_reduce(rmax[:], rt1[:], AX.X, ALU.add))
                dve.tensor_copy(pos_i[:], rmax[:]).then_inc(r_pos, 1)
                se = (P, NSLOT + 1, E1)
                link(dve.tensor_tensor(cse[:], ends[:].unsqueeze(1).to_broadcast(se), s_io[:].unsqueeze(2).to_broadcast(se),
                                       ALU.is_le))
                link(dve.tensor_reduce(sef[:], cse[:], AX.X, ALU.add))
                dve.tensor_scalar(out=slot_e[:], in0=sef[:], scalar1=float(E1 - 1), scalar2=None,
                                  op0=ALU.min).then_inc(r_slot, 1)

            def step(g, i):
                n = MC * g + i
                m, c = divmod(i, DC)
                if not zero(g):
                    dve.wait_ge(act_g, 3 * n + 2)
                    dve.tensor_tensor(xs_b[:, i % 2, :], act_o[:, i % 2, 0, :], act_o[:, i % 2, 1, :],
                                      ALU.mult).then_inc(xs_ok, 1)
                dve.wait_ge(a_ok, n + 1)
                dve.wait_ge(xs_ok, n + 1)
                if not zero(g):
                    dve.wait_ge(hst, n - MC + 1)
                dve.tensor_tensor_scan(h_b[:, i % 2, :], a_b[:, i % 2, :], xs_b[:, i % 2, :], hstate[:, i:i + 1],
                                       ALU.mult, ALU.add).then_inc(scan_ok, 1)
                dve.wait_ge(scan_ok, n + 1)
                dve.tensor_copy(hstate[:, i:i + 1], h_b[:, i % 2, GT - 1:GT]).then_inc(hst, 1)
                if i == 0:
                    dve.wait_ge(comb_in, 16 * (g + 1))
                if i >= 4:
                    dve.wait_ge(acc_ok, 6 * g + i - 3)
                elif not zero(g):
                    dve.wait_ge(acc_ok, 6 * g)
                dst = accO[:, c, :] if m == 0 else hw_b[:, i % 2, :]
                dve.tensor_tensor(dst.rearrange("p (t q) -> p t q", q=P),
                                  h_b[:, i % 2, :].rearrange("p (t q) -> p t q", q=P),
                                  comb_b[:, bass.ds(ring(g), 1), :, m, :].rearrange("p a t q -> p (a t) q"),
                                  ALU.mult).then_inc(hw_ok, 1)

            def total(g):
                dve.wait_ge(x1b_in, 16 * (g + 1))
                if isinstance(g, int) and g < B_FIRST - 1:
                    dve.wait_ge(fin_full, g + 1)
                    dve.tensor_tensor(first_res[:, g], side4, x1_b[:], ALU.add).then_inc(fin_ok, 1)
                    return
                dve.wait_ge(y_in, 64 * (g - 1))
                dve.tensor_tensor(x1_b[:], x1_b[:], y_b[:], ALU.add).then_inc(fin_sum, 1)
                dve.wait_ge(fin_sum, g - 1)
                dve.wait_ge(fin_full, g + 1)
                if isinstance(g, int) and g == GROUPS - 1:
                    for j in (0, 2):
                        dve.tensor_tensor(x1_b[:, j:j + 2, :], side4[:, j:j + 2, :], x1_b[:, j:j + 2, :],
                                          ALU.add).then_inc(fin_ok, 1)
                else:
                    dve.tensor_tensor(x1_b[:], side4, x1_b[:], ALU.add).then_inc(fin_ok, 1)

            def w1_half(s, h):
                dve.wait_ge(w1_hi, 2 * s + h + 1)
                f = slice(h * HALF1, (h + 1) * HALF1)
                dve.tensor_tensor(w1_l[:, :, f], raw1[:, :, f], w1_h[:, :, f].bitcast(F32), ALU.subtract).then_inc(w1_lo, 1)

            def rows_lo(s):
                dve.wait_ge(sT_hi, s + 1)
                dve.tensor_tensor(sT_l[:].rearrange("p c t -> p (c t)"), ps[:, 6, :],
                                  sT_h[:].rearrange("p c t -> p (c t)").bitcast(F32), ALU.subtract).then_inc(sT_ok, 1)

            def parts(s, q):
                n = FJ // 2 * s + q
                dve.wait_ge(t_ok, 2 * (n + 1))
                j = slice(2 * q, 2 * q + 2)
                dve.tensor_copy(eT_h[:, j, :], t32[:, j, :]).then_inc(e_hi, 1)
                dve.wait_ge(e_hi, n + 1)
                dve.tensor_tensor(eT_l[:, j, :], t32[:, j, :], eT_h[:, j, :].bitcast(F32), ALU.subtract).then_inc(e_ok, 1)

            def slot(s, last=False):
                for q in range(FJ // 2):
                    parts(s, q)
                if not last:
                    rows_lo(s + 1)
                    w1_half(s + 1, 0)
                    w1_half(s + 1, 1)
                dve.wait_ge(b2_in, 16 * (s + 1))
                if not zero(s):
                    dve.wait_ge(y_st, 16 * s)
                dve.wait_ge(l2_full, s + 1)
                dve.tensor_tensor(y_sb[:], ps[:, 4:6, 0:D], b2b[:].unsqueeze(1).to_broadcast((P, ST, D)),
                                  ALU.add).then_inc(ys_ok, 1)

            g = GROUPS - 1
            for tiles in (range(0, 2), range(2, 4)):
                ln1_stats(dve, g, tiles)
            ln_aggr(dve, stats1, mv1, bn1, mvs1, g)
            ln1_norm(dve, g, range(JT))
            for i in range(MC):
                if i == 3:
                    lo_of(dve, post_use(g, "t1")[1], nT_l[:], nT_h[:], side2)
                step(0, i)
                for n in LO_LATE_M3.get(i, []):
                    split_late(n)
                if i == 5:
                    gate_logits(dve, g)
                    choose_expert()
                    mixture_weights(dve, link, mix2)
                if i == 6:
                    mixture_finish(dve, link, mix2, 2)
            for g in range(1, B_FIRST):
                for i in range(MC):
                    step(g, i)
                    if g == 1 and i == 0:
                        slot_rows()
                    if i == rows_step(g) + 1:
                        total(g - 1)
                    if g == B_FIRST - 1 and i in (5, 6):
                        w1_half(0, i - 5)
                    if g == B_FIRST - 1 and i == MC - 2:
                        rows_lo(0)
            slot(0)
            with dve.Fori(1, NSLOT - 1) as s:
                slot(s)
            slot(NSLOT - 1, True)
            with dve.Fori(B_FIRST, GROUPS - 1) as g:
                for i in range(MC):
                    step(g, i)
                    if i == rows_step(g) + 1:
                        total(g - 1)
            g = GROUPS - 1
            for i in range(MC):
                step(g, i)
                if i == rows_step(g) + 1:
                    total(g - 1)
                if i in (5, 6):
                    if i == 5:
                        dve.wait_ge(first_y_in, 2 * 64)
                    dve.tensor_tensor(first_res[:, i - 5], first_res[:, i - 5], first_y[:, i - 5],
                                      ALU.add).then_inc(first_ok, 1)
            total(g)


def kernel(**inputs):
    import concourse.bacc as bacc
    from concourse.bass_utils import run_bass_kernel_spmd

    def c(x):
        return np.ascontiguousarray(x)

    i = inputs
    host = {
        "x": c(i["L0_attn_x"]),
        "wqk": c(np.stack([i["L0_attn_W_q"], i["L0_attn_W_k"]])),
        "wg": c(i["L0_attn_W_g"].T),
        "wv": c(np.concatenate([i["L0_attn_W_v"].T, i["L0_ffn_expert_sel"].T], axis=1)),
        "wo": c(i["L0_attn_W_o"].T),
        "log_decay": c(i["L0_attn_log_decay"]),
        "keys": c(np.transpose(i["L0_ffn_keys"], (1, 0, 2)).reshape(D, E0 * H0)),
        "values": c(i["L0_ffn_values"]),
        "wgvd": c(np.stack([i["L1_attn_Wg"], i["L1_attn_Wv"], i["L1_attn_Wd"]])),
        "scan_bias": c(np.stack([i["L1_attn_bg"], i["L1_attn_bv"], i["L1_attn_bd"]]).reshape(3, MC, P).transpose(2, 0, 1)),
        "gates": c(np.concatenate([i["L1_attn_gate_W"], i["L1_ffn_gate_w"].T], axis=1)),
        "gate_b": c(i["L1_ffn_gate_b"]),
        "expert_bias": c(i["L1_ffn_expert_bias"]),
        "w1": c(i["L1_ffn_w1"]),
        "b1": c(i["L1_ffn_b1"].reshape(E1, FJ, P).transpose(0, 2, 1)),
        "w2": c(i["L1_ffn_w2"]),
        "b2": c(i["L1_ffn_b2"]),
    }
    nc = bacc.Bacc("TRN2", target_bir_lowering=False, num_devices=1)
    aps = {n: nc.dram_tensor(n, v.shape, mybir.dt.from_np(v.dtype), kind="ExternalInput").ap() for n, v in host.items()}
    out = nc.dram_tensor("out", (1, T, D), F32, kind="ExternalOutput").ap()
    build(nc, aps, out)
    r = run_bass_kernel_spmd(nc, [host], core_ids=[0])
    return r.results[0]["out"]
```
